# Optimizing a Trainium2 kernel written in Bass

```python
import numpy as np
import jax
import jax.numpy as jnp

def _softmax(x, axis=-1):
    return jax.nn.softmax(x, axis=axis)

def _gelu(x):
    return jax.nn.gelu(x, approximate=True)

def _silu(x):
    return jax.nn.silu(x)

def _sigmoid(x):
    return jax.nn.sigmoid(x)

def _layernorm(x, axis=-1, eps=1e-05):
    m = jnp.mean(x, axis=axis, keepdims=True)
    v = jnp.var(x, axis=axis, keepdims=True)
    return (x - m) / jnp.sqrt(v + eps)

def _scatter_add(tgt, idx, src, axis=0):
    return tgt.at[idx].add(src)

def _segment_sum(src, seg, n):
    return jax.ops.segment_sum(src, seg, n)
kernel_name = 'mk_vit_tower_d1_tok_img1024_r4_948af3'

def setup_inputs(seed: int=0):
    np.random.seed(seed)
    _w = jnp.asarray

    def _rec_inputs():
        import jax
        import jax.numpy as jnp
        _rk = jax.random.key(seed)
        x = -0.00016672 + 0.999947 * jax.random.normal(jax.random.fold_in(_rk, 1), (16, 3, 96, 96), jnp.float32)
        return x
    x = _rec_inputs()

    def _L0_tok_setup():
        import jax, jax.numpy as jnp
        import numpy as np
        PATCH = 16

        def _patchify(x, p):
            B, C, H, W = x.shape
            nh, nw = (H // p, W // p)
            x = x.reshape(B, C, nh, p, nw, p)
            x = x.transpose(0, 2, 4, 1, 3, 5)
            return x.reshape(B, nh * nw, C * p * p)
        key = jax.random.key(seed)
        k1, k2, k3, k4, k5 = jax.random.split(key, 5)
        B, C, H = (64, 3, 96)
        d_model = 256
        p = PATCH
        num_patches = (H // p) ** 2
        in_dim = p * p * C
        x = jax.random.normal(k1, (B, C, H, H), dtype=jnp.float32)
        bound = 1.0 / np.sqrt(in_dim)
        W = jax.random.uniform(k2, (d_model, in_dim), dtype=jnp.float32, minval=-bound, maxval=bound)
        b = jax.random.uniform(k3, (d_model,), dtype=jnp.float32, minval=-bound, maxval=bound)
        cls_token = jax.random.normal(k4, (1, 1, d_model), dtype=jnp.float32)
        pos_enc = jax.random.normal(k5, (1, num_patches + 1, d_model), dtype=jnp.float32)
        return {'x': x, 'W': W, 'b': b, 'cls_token': cls_token, 'pos_enc': pos_enc}
    _L0_tok_all = _L0_tok_setup()
    _L0_tok_in = {k: v for k, v in _L0_tok_all.items() if k in ('W', 'b', 'cls_token', 'pos_enc')}
    del _L0_tok_all

    def _L0_attn_setup():
        import jax, jax.numpy as jnp
        import numpy as np
        import math
        DIM = 256
        THETA = 10000.0

        def rope_cos_sin(seq_len, dim, dtype=jnp.float32):
            inv = 1.0 / THETA ** (jnp.arange(0, dim, 2, dtype=jnp.float32) / dim)
            t = jnp.arange(seq_len, dtype=jnp.float32)
            ang = jnp.outer(t, inv)
            return (jnp.cos(ang).astype(dtype), jnp.sin(ang).astype(dtype))

        def apply_rotary(x, cos, sin):
            B, S, D = x.shape
            xr = x[..., 0::2]
            xi = x[..., 1::2]
            or_ = xr * cos - xi * sin
            oi_ = xr * sin + xi * cos
            return jnp.stack([or_, oi_], axis=-1).reshape(B, S, D)
        key = jax.random.key(seed)
        ks = jax.random.split(key, 5)
        B, S, D = (4, 512, DIM)
        x = jax.random.normal(ks[0], (B, S, D), dtype=jnp.float32)
        s = 1.0 / math.sqrt(D)
        wq = jax.random.normal(ks[1], (D, D), dtype=jnp.float32) * s
        wk = jax.random.normal(ks[2], (D, D), dtype=jnp.float32) * s
        wv = jax.random.normal(ks[3], (D, D), dtype=jnp.float32) * s
        wo = jax.random.normal(ks[4], (D, D), dtype=jnp.float32) * s
        return {'x': x, 'wq': wq, 'wk': wk, 'wv': wv, 'wo': wo}
    _L0_attn_all = _L0_attn_setup()
    _L0_attn_in = {k: v for k, v in _L0_attn_all.items() if k in ('wq', 'wk', 'wv', 'wo')}
    del _L0_attn_all

    def _L0_ffn_setup():
        import jax, jax.numpy as jnp
        import numpy as np
        E = 8
        TOPK = 2
        SCALE = 2.0
        key = jax.random.key(seed)
        ks = jax.random.split(key, 12)
        B, S, D, F, R = (2, 128, 256, 1024, 16)
        w = lambda k, shp: jax.random.normal(k, shp, dtype=jnp.float32) * 0.02
        return {'hidden_states': jax.random.normal(ks[0], (B, S, D), dtype=jnp.float32), 'gate_w': w(ks[1], (E, D)), 'w_gate': w(ks[2], (F, D)), 'w_up': w(ks[3], (F, D)), 'w_down': w(ks[4], (D, F)), 'A1': w(ks[5], (E, R, D)), 'B1': w(ks[6], (E, F, R)), 'A3': w(ks[7], (E, R, D)), 'B3': w(ks[8], (E, F, R)), 'A2': w(ks[9], (E, R, F)), 'B2': w(ks[10], (E, D, R))}
    _L0_ffn_all = _L0_ffn_setup()
    _L0_ffn_in = {k: v for k, v in _L0_ffn_all.items() if k in ('gate_w', 'w_gate', 'w_up', 'w_down', 'A1', 'B1', 'A3', 'B3', 'A2', 'B2')}
    del _L0_ffn_all
    return {'x': x, 'L0_tok_W': _L0_tok_in['W'], 'L0_tok_b': _L0_tok_in['b'], 'L0_tok_cls_token': _L0_tok_in['cls_token'], 'L0_tok_pos_enc': _L0_tok_in['pos_enc'], 'L0_attn_wq': _L0_attn_in['wq'], 'L0_attn_wk': _L0_attn_in['wk'], 'L0_attn_wv': _L0_attn_in['wv'], 'L0_attn_wo': _L0_attn_in['wo'], 'L0_ffn_gate_w': _L0_ffn_in['gate_w'], 'L0_ffn_w_gate': _L0_ffn_in['w_gate'], 'L0_ffn_w_up': _L0_ffn_in['w_up'], 'L0_ffn_w_down': _L0_ffn_in['w_down'], 'L0_ffn_A1': _L0_ffn_in['A1'], 'L0_ffn_B1': _L0_ffn_in['B1'], 'L0_ffn_A3': _L0_ffn_in['A3'], 'L0_ffn_B3': _L0_ffn_in['B3'], 'L0_ffn_A2': _L0_ffn_in['A2'], 'L0_ffn_B2': _L0_ffn_in['B2']}

def reference(x, L0_tok_W, L0_tok_b, L0_tok_cls_token, L0_tok_pos_enc, L0_attn_wq, L0_attn_wk, L0_attn_wv, L0_attn_wo, L0_ffn_gate_w, L0_ffn_w_gate, L0_ffn_w_up, L0_ffn_w_down, L0_ffn_A1, L0_ffn_B1, L0_ffn_A3, L0_ffn_B3, L0_ffn_A2, L0_ffn_B2):
    import jax
    import jax.numpy as jnp

    def _L0_tok_ref(x, W, b, cls_token, pos_enc):
        import jax, jax.numpy as jnp
        import numpy as np
        PATCH = 16

        def _patchify(x, p):
            B, C, H, W = x.shape
            nh, nw = (H // p, W // p)
            x = x.reshape(B, C, nh, p, nw, p)
            x = x.transpose(0, 2, 4, 1, 3, 5)
            return x.reshape(B, nh * nw, C * p * p)
        B = x.shape[0]
        patches = _patchify(x, PATCH)
        proj = jnp.einsum('bnf,df->bnd', patches, W) + b
        cls = jnp.broadcast_to(cls_token, (B, 1, cls_token.shape[-1]))
        out = jnp.concatenate([cls, proj], axis=1) + pos_enc
        return out

    def _L0_attn_ref(x, wq, wk, wv, wo):
        import jax, jax.numpy as jnp
        import numpy as np
        import math
        DIM = 256
        THETA = 10000.0

        def rope_cos_sin(seq_len, dim, dtype=jnp.float32):
            inv = 1.0 / THETA ** (jnp.arange(0, dim, 2, dtype=jnp.float32) / dim)
            t = jnp.arange(seq_len, dtype=jnp.float32)
            ang = jnp.outer(t, inv)
            return (jnp.cos(ang).astype(dtype), jnp.sin(ang).astype(dtype))

        def apply_rotary(x, cos, sin):
            B, S, D = x.shape
            xr = x[..., 0::2]
            xi = x[..., 1::2]
            or_ = xr * cos - xi * sin
            oi_ = xr * sin + xi * cos
            return jnp.stack([or_, oi_], axis=-1).reshape(B, S, D)
        B, S, D = x.shape
        xq = jnp.einsum('bsd,ed->bse', x, wq)
        xk = jnp.einsum('bsd,ed->bse', x, wk)
        xv = jnp.einsum('bsd,ed->bse', x, wv)
        cos, sin = rope_cos_sin(S, D, x.dtype)
        xq = apply_rotary(xq, cos, sin)
        xk = apply_rotary(xk, cos, sin)
        scores = jnp.einsum('bqd,bkd->bqk', xq, xk) / jnp.sqrt(jnp.asarray(D, x.dtype))
        attn = jax.nn.softmax(scores, axis=-1)
        out = jnp.einsum('bqk,bkd->bqd', attn, xv)
        return jnp.einsum('bsd,ed->bse', out, wo)

    def _L0_ffn_ref(hidden_states, gate_w, w_gate, w_up, w_down, A1, B1, A3, B3, A2, B2):
        import jax, jax.numpy as jnp
        import numpy as np
        E = 8
        TOPK = 2
        SCALE = 2.0
        B, S, D = hidden_states.shape
        x = hidden_states.reshape(-1, D)
        N = x.shape[0]
        probs = jax.nn.softmax(x @ gate_w.T, axis=-1)
        vals, idx = jax.lax.top_k(probs, TOPK)
        rw = vals / jnp.sum(vals, axis=-1, keepdims=True)
        weight = jnp.zeros((N, E), x.dtype).at[jnp.arange(N)[:, None], idx].add(rw)
        common_w1 = x @ w_gate.T
        common_w3 = x @ w_up.T
        d1 = jnp.einsum('enr,efr->enf', jnp.einsum('nd,erd->enr', x, A1), B1) * SCALE
        d3 = jnp.einsum('enr,efr->enf', jnp.einsum('nd,erd->enr', x, A3), B3) * SCALE
        act = jax.nn.silu(common_w1[None] + d1) * (common_w3[None] + d3)
        out = jnp.einsum('ne,enf->nf', weight, act) @ w_down.T
        z = jnp.einsum('enf,erf->enr', act, A2)
        out = out + jnp.einsum('ne,enr,edr->nd', weight, z, B2) * SCALE
        return out.reshape(B, S, D)
    h = _L0_tok_ref(x, L0_tok_W, L0_tok_b, L0_tok_cls_token, L0_tok_pos_enc)
    h = h + _L0_attn_ref(_layernorm(h, axis=-1), L0_attn_wq, L0_attn_wk, L0_attn_wv, L0_attn_wo)
    h = h + _L0_ffn_ref(_layernorm(h, axis=-1), L0_ffn_gate_w, L0_ffn_w_gate, L0_ffn_w_up, L0_ffn_w_down, L0_ffn_A1, L0_ffn_B1, L0_ffn_A3, L0_ffn_B3, L0_ffn_A2, L0_ffn_B2)
    return h

_drawn_inputs = setup_inputs


def setup_inputs(seed=0):
    import zlib

    import numpy as np

    out = dict(_drawn_inputs(seed))
    spreads = {}
    factors = {'L0_ffn_gate_w': 8.0,
     'L0_ffn_A1': 8.0,
     'L0_ffn_B1': 8.0,
     'L0_ffn_A3': 8.0,
     'L0_ffn_B3': 8.0,
     'L0_ffn_A2': 8.0,
     'L0_ffn_B2': 8.0}
    for name, (base, spread) in spreads.items():
        noise = np.random.default_rng([zlib.crc32(name.encode()), seed]).standard_normal(out[name].shape)
        drawn = base * np.exp(spread * noise) if base else spread * noise
        out[name] = jnp.asarray(drawn.astype(out[name].dtype))
    for name, factor in factors.items():
        out[name] = (out[name] * factor).astype(out[name].dtype)
    return out
```

```python
from contextlib import ExitStack

import numpy as np
import concourse.bass as bass
from concourse import mybir

ALU = mybir.AluOpType
ACT = mybir.ActivationFunctionType
AX_X = mybir.AxisListType.X
F32 = mybir.dt.float32
F32R = mybir.dt.float32r
BF16 = mybir.dt.bfloat16

P = 128
IMAGES, CHANNELS, SIDE, PATCH = 16, 3, 96, 16
D = 256
F = 1024
EXPERTS, RANK = 8, 16
GRID = SIDE // PATCH
ROWS = GRID * GRID + 1
HALVES = 2
HALF_IMAGES = IMAGES // HALVES
GROUP_IMAGES = 3
GROUPS = -(-HALF_IMAGES // GROUP_IMAGES)
GR = GROUP_IMAGES * ROWS
GRE = GR + 1
HT = HALF_IMAGES * ROWS
HP = GROUPS * GR
HPE = HP + 1
KX = CHANNELS * PATCH * PATCH // P
KD = D // P
FT = F // P
EPS = 1e-5
SCORE_SCALE = float(D) ** -0.5
LORA_SCALE = 2.0
FAR = -1e30
TAKEN = -3e38

C_ID, C_MASK = 0, P
C_COS = C_MASK + GRE
C_SIN = C_COS + ROWS
C_RANK = C_SIN + ROWS
C_ALL = C_RANK + EXPERTS
M_QK = 0
M_A13 = M_QK + KD * 4 * P
M_GATE = M_A13 + KD * 2 * P
M_B2 = M_GATE + KD * EXPERTS
M_ALL = M_B2 + KD * P
T_UP = 0
T_B13 = T_UP + 2 * KD * P
T_A2 = T_B13 + 2 * P
T_DOWN = T_A2 + P
T_ALL = T_DOWN + KD * P
CHUNK_TILES = 2
CHUNKS = FT // CHUNK_TILES
STAGE = CHUNK_TILES * T_ALL


def vit_block(nc, patches, embed_w, value_w, small_w, ffn_w, const, table, out):
    ctx = ExitStack()
    with ctx:
        def sb(name, shape, dt=F32, where=ctx):
            return where.enter_context(nc.sbuf_tensor(name, shape, dt))

        def pair(name, cols, where=ctx):
            return [sb(f"{name}_{part}", [P, cols], F32R, where) for part in ("hi", "lo")]

        def sem(name):
            return ctx.enter_context(nc.semaphore(name))

        def as_f32(ap):
            return ap.bitcast(F32)

        cst = sb("cst", [P, C_ALL])
        tab = sb("tab", [GR, 2, D])
        add_rows = sb("add_rows", [GR, D])
        stage = [sb(f"stage{i}", [P, STAGE]) for i in range(3)]
        small = pair("small", M_ALL)
        vo = pair("vo", KD * D)
        chunk = [pair(f"chunk{c}", STAGE) for c in range(2)]
        resid = [sb(f"resid{h}", [GR, GROUPS, D]) for h in range(HALVES)]
        xnorm = sb("xnorm", [GR, GROUPS, D])
        xT = [pair(f"xT{h}", KD * HPE) for h in range(HALVES)]
        ident_bf = sb("ident_bf", [P, P], BF16)
        minus_half = sb("minus_half", [GR, GROUPS])
        stats = sb("stats", [GR, GROUPS, 6])
        moments = sb("moments", [GR, GROUPS, 2])
        spread = sb("spread", [GR, GROUPS])
        rstd = sb("rstd", [GR, GROUPS])

        with ExitStack() as early:
            xhalf = [pair(f"xhalf{h}", KX * HP, early) for h in range(HALVES)]
            embed = pair("embed", KX * D, early)
            valout = pair("valout", 2 * KD * D, early)
        chunk += [pair(f"chunk{c}", STAGE) for c in range(2, CHUNKS)]
        with ExitStack() as attn:
            rot = [sb(f"rot{i}", [P, 2, HT], F32, attn) for i in range(4)]
            qk = pair("qk", 4 * HPE, attn)
            val = [pair(f"val{h}", GROUPS * D, attn) for h in range(HALVES)]
            scores = sb("scores", [GR, GROUPS, GRE], F32, attn)
            probs = sb("probs", [GR, GROUPS, GRE], F32, attn)
            probsT = pair("probsT", HP, attn)
            top = sb("top", [GR, GROUPS], F32, attn)
            neg_top = sb("neg_top", [GR, GROUPS], F32, attn)
            total = sb("total", [GR, GROUPS], F32, attn)
            inv_total = sb("inv_total", [GR, GROUPS], F32, attn)
        logits = sb("logits", [GR, GROUPS, EXPERTS])
        logits2 = sb("logits2", [GR, GROUPS, EXPERTS])
        hits = sb("hits", [GR, GROUPS, EXPERTS])
        first = sb("first", [GR, GROUPS])
        best = sb("best", [GR, 2, GROUPS])
        gap = sb("gap", [GR, GROUPS])
        gap_exp = sb("gap_exp", [GR, GROUPS])
        gap_den = sb("gap_den", [GR, GROUPS])
        chosen = [sb(f"chosen{s}", [GR, GROUPS, EXPERTS]) for s in range(2)]
        slot_w = sb("slot_w", [GR, 2, GROUPS])
        chosen_x = sb("chosen_x", [GR, 2, GROUPS, EXPERTS, RANK], BF16)
        slot_wx = sb("slot_wx", [GR, 2, GROUPS, P])
        ranks = [sb(f"ranks{h}", [P, 2, HT]) for h in range(HALVES)]
        mask = sb("mask", [P, 2, HT])
        weight = sb("weight", [P, 2, HT])
        slot_in = sb("slot_in", [P, 2, 2, HT])
        slot_inr = pair("slot_inr", 4 * HT)
        act_ring = sb("act_ring", [P, 3, 2, HT])
        actr = [pair(f"actr{i}", 2 * HT) for i in range(2)]
        mix_ring = sb("mix_ring", [P, 2, HT])
        mixr = [pair(f"mixr{i}", HT) for i in range(2)]
        low = sb("low", [P, 2, HT])
        low_sum = sb("low_sum", [P, HT])
        lowr = pair("lowr", HT)
        yT = sb("yT", [P, KD, HT])

        bank = [ctx.enter_context(nc.psum_tensor(f"bank{i}", [P, 512], F32)) for i in range(4)]
        rope_banks = ctx.enter_context(nc.psum_tensor("rope_banks", [P, 4, 512], F32))
        bank += [rope_banks[:, i, :] for i in range(4)]

        half_x = KX // 2 * HP
        half_w = KX // 2 * D
        LOADS = [
            ("w_a", 1, 0, embed_w[:, 0:half_w], [e[:, 0:half_w] for e in embed]),
            ("x0_a", 2, 0, patches[:, 0, 0:half_x], [x[:, 0:half_x] for x in xhalf[0]]),
            ("w_b", 1, half_w, embed_w[:, half_w:], [e[:, half_w:] for e in embed]),
            ("x0_b", 2, half_x, patches[:, 0, half_x:], [x[:, half_x:] for x in xhalf[0]]),
            ("x1", 0, 0, patches[:, 1, :], [x[:] for x in xhalf[1]]),
            ("valout", 1, 0, value_w, [v[:] for v in valout]),
            ("small", 2, 0, small_w, [s[:] for s in small]),
        ] + [(f"ffn{c}", c % 3, 0, ffn_w[:, c, :], [w[:] for w in chunk[c]]) for c in range(CHUNKS)]
        load_at = {name: (stage[slot][:, off:off + src.shape[1]], src, parts)
                   for name, slot, off, src, parts in LOADS}
        FREES = {"valout": ("w_a", "w_b"), "small": ("x0_a", "x0_b"), "ffn0": ("x1",),
                 "ffn1": ("valout",), "ffn2": ("small",), "ffn3": ("ffn0",)}
        loaded = {name: sem(f"loaded_{name}") for name, *_ in LOADS}
        hi_done = {name: sem(f"hi_{name}") for name, *_ in LOADS}
        lo_done = {name: sem(f"lo_{name}") for name, *_ in LOADS}

        s_const = sem("const_loaded")
        s_table = sem("table_loaded")
        s_rows = sem("add_rows_ready")
        s_ident = sem("ident_bf_ready")
        s_pads = sem("pads_cleared")
        s_mhalf = sem("minus_half_ready")
        tok_done = sem("tok_done")
        resid_ready = sem("resid_ready")
        vo_mm, vo_hi, vo_lo = sem("vo_mm"), sem("vo_hi_ready"), sem("vo_lo_ready")
        moments_ready = sem("moments_ready")
        spread_ready = sem("spread_ready")
        rstd_ready = sem("rstd_ready")
        xnorm_ready = sem("xnorm_ready")
        xT_mm = sem("xT_mm")
        xT_hi = sem("xT_hi_ready")
        xT_lo = sem("xT_lo_ready")
        qk_mm = sem("qk_mm")
        rot_read = sem("rot_read")
        rot_even = sem("rot_even_ready")
        rot_odd = sem("rot_odd_ready")
        qk_hi = sem("qk_hi_ready")
        qk_lo = sem("qk_lo_ready")
        v_mm, v_hi, v_lo = sem("v_mm"), sem("v_hi_ready"), sem("v_lo_ready")
        s_mm, s_masked, s_negtop = sem("scores_mm"), sem("scores_masked"), sem("neg_top_ready")
        p_ready, inv_ready = sem("probs_ready"), sem("inv_total_ready")
        pT_mm, pT_hi, pT_lo = sem("pT_mm"), sem("pT_hi_ready"), sem("pT_lo_ready")
        pv_mm = sem("pv_mm")
        h2_ready = sem("h2_ready")
        gate_mm = sem("gate_mm")
        logits_ready = sem("logits_ready")
        gap_ready, gap_exp_ready = sem("gap_ready"), sem("gap_exp_ready")
        ranks_ready = sem("ranks_ready")
        slots_ready = sem("slots_ready")
        expand_mm = sem("expand_mm")
        mask_ready, weight_ready = sem("mask_ready"), sem("weight_ready")
        slot_in_ready = sem("slot_in_ready")
        slot_hi, slot_lo = sem("slot_hi_ready"), sem("slot_lo_ready")
        up1_mm, up2_mm = sem("up1_mm"), sem("up2_mm")
        silu1, silu2 = sem("silu1_done"), sem("silu2_done")
        act1, act2 = sem("act1_done"), sem("act2_done")
        actw, act_hi, act_lo = sem("act_weighted"), sem("act_hi_ready"), sem("act_lo_ready")
        mixed, mix_hi, mix_lo = sem("mixed"), sem("mix_hi_ready"), sem("mix_lo_ready")
        down_mm = sem("down_mm")
        low_ready, low_hi, low_lo = sem("low_ready"), sem("low_hi_ready"), sem("low_lo_ready")
        y_mm = sem("y_mm")
        y_act, y_dve = sem("y_act_copied"), sem("y_dve_copied")
        s_out = sem("stored")
        s_chain = sem("dve_chain")
        s_act_chain = sem("act_chain")
        s_pool_chain = sem("pool_chain")

        NS = HALVES * FT
        ident = cst[:, C_ID:C_ID + P]
        far_mask = cst[0:GR, C_MASK:C_MASK + GRE]

        def up_banks(n):
            return bank[2 * (n % 2)], bank[2 * (n % 2) + 1]

        def v_banks(h, g):
            lo_bank, hi_bank = ((bank[0], bank[3]), (bank[6], bank[7]))[h]
            b = lo_bank if g < 2 else hi_bank
            return b[0:GR, (g % 2) * D:(g % 2) * D + D]

        def xT_bank(n, k):
            return bank[(1 if n < 2 else 4) + k]

        def rank_bank(h, w):
            return ((bank[0], bank[3]), (bank[6], bank[7]))[h][w]

        def ffn_w_at(part, t, at, cols=P):
            base = (t % CHUNK_TILES) * T_ALL + at
            return chunk[t // CHUNK_TILES][part][:, base:base + cols]

        block = ctx.enter_context(nc.Block())

        @block.sync
        def _(sp):
            for name, *_ in LOADS:
                for earlier in FREES.get(name, ()):
                    sp.wait_ge(hi_done[earlier], 1)
                    sp.wait_ge(lo_done[earlier], 1)
                slot, src, _parts = load_at[name]
                sp.dma_start(slot, src).then_inc(loaded[name], 16)
            for h in range(HALVES):
                sp.wait_ge(y_act, h + 1)
                sp.wait_ge(y_dve, h + 1)
                sp.dma_start(out[:, h, :, :], yT[:, :, :]).then_inc(s_out, 16)
            sp.wait_ge(s_out, 16 * HALVES)

        @block.gpsimd
        def _(pool):
            nc.gpsimd.memset(minus_half[:], -0.5).then_inc(s_mhalf, 1)

            def inv_std(n):
                pool.wait_ge(moments_ready, GROUPS * (n + 1))
                nc.gpsimd.tensor_scalar(spread[:], moments[:, :, 1], EPS, None, ALU.add).then_inc(spread_ready, 1)
                pool.wait_ge(spread_ready, n + 1)
                nc.gpsimd.tensor_tensor(rstd[:], spread[:], minus_half[:], ALU.pow).then_inc(rstd_ready, 1)

            def lo_part(name):
                pool.wait_ge(hi_done[name], 1)
                slot, _src, (hi, lo) = load_at[name]
                nc.gpsimd.tensor_tensor(lo, slot, as_f32(hi), ALU.subtract).then_inc(lo_done[name], 1)

            pool.wait_ge(s_mhalf, 1)
            inv_std(0)
            inv_std(1)
            pool.wait_ge(vo_mm, 1)
            for i in range(4):
                for part in qk:
                    pad = part[:, i * HPE + HT:(i + 1) * HPE].bitcast(F32)
                    last = nc.gpsimd.memset(pad, 0.0)
            last.then_inc(s_pads, 1)
            for c in range(CHUNKS - 1):
                lo_part(f"ffn{c}")
            inv_std(2)
            inv_std(3)
            lo_part(f"ffn{CHUNKS - 1}")

            for n in range(NS):
                pool.wait_ge(actw, n + 1)
                if n >= 2:
                    pool.wait_ge(mix_hi, n - 1)
                    pool.wait_ge(mix_lo, n - 1)
                nc.gpsimd.tensor_tensor(mix_ring[:, n % 2, :], act_ring[:, n % 3, 0, :],
                                        act_ring[:, n % 3, 1, :], ALU.add).then_inc(mixed, 1)

        @block.scalar
        def _(act):
            act.dma_start(cst[:], const).then_inc(s_const, 16)
            act.dma_start(tab[:], table).then_inc(s_table, 16)

            def hi_part(name):
                act.wait_ge(loaded[name], 16)
                if name == "ffn2":
                    act.wait_ge(vo_mm, 1)
                slot, _src, (hi, _lo) = load_at[name]
                nc.scalar.activation(hi, slot, ACT.Copy).then_inc(hi_done[name], 1)

            def xT_hi_part(n):
                act.wait_ge(xT_mm, n + 1)
                for k in range(KD):
                    last = nc.scalar.activation(xT[n % 2][0][:, k * HPE:k * HPE + HP],
                                                xT_bank(n, k)[:, 0:HP], ACT.Copy)
                    last.then_inc(xT_hi, 1)

            def v_hi_part(h):
                act.wait_ge(v_mm, h + 1)
                for g in range(GROUPS):
                    nc.scalar.activation(val[h][0][0:GR, g * D:(g + 1) * D], v_banks(h, g), ACT.Copy).then_inc(v_hi, 1)

            def qk_hi_part(h):
                if h:
                    act.wait_ge(s_mm, h)
                for i, ready in enumerate((rot_even, rot_odd)):
                    act.wait_ge(ready, h + 1)
                    dst = qk[0][:].rearrange("p (i t) -> p i t", i=4)[:, 2 * i:2 * i + 2, 0:HT]
                    nc.scalar.activation(dst, rot[2 * i][:], ACT.Copy).then_inc(qk_hi, 1)

            def exp_scores(h):
                act.wait_ge(s_negtop, h + 1)
                if h:
                    act.wait_ge(pT_mm, h)
                    act.wait_ge(inv_ready, h)
                for g in range(GROUPS):
                    last = nc.scalar.activation(probs[:, g, :], scores[:, g, :], ACT.Exp, bias=neg_top[:, g:g + 1],
                                                scale=SCORE_SCALE, accum_out=total[:, g:g + 1])
                    last.then_inc(p_ready, 1)

            def pT_hi_part(h):
                act.wait_ge(pT_mm, h + 1)
                if h:
                    act.wait_ge(pv_mm, h)
                nc.scalar.activation(probsT[0][0:GR, :], bank[2][0:GR, 0:HP], ACT.Copy).then_inc(pT_hi, 1)

            def expand(h):
                act.wait_ge(expand_mm, h + 1)
                if h:
                    act.wait_ge(actw, FT)
                    act.wait_ge(low_ready, 1)
                for s in range(2):
                    nc.scalar.activation(mask[:, s, :], bank[s][:, 0:HT], ACT.Copy).then_inc(mask_ready, 1)
                for s in range(2):
                    nc.scalar.activation(weight[:, s, :], bank[2 + s][:, 0:HT], ACT.Copy).then_inc(weight_ready, 1)
                act.wait_ge(slot_in_ready, 3 * (h + 1))
                if h:
                    act.wait_ge(up2_mm, FT)
                nc.scalar.activation(slot_inr[0][:], slot_in[:].rearrange("p s w t -> p (s w t)"),
                                     ACT.Copy).then_inc(slot_hi, 1)

            def silu(n, slot):
                act.wait_ge((up1_mm, up2_mm)[slot], n + 1)
                if n >= 3 and slot == 0:
                    act.wait_ge(mixed, n - 2)
                    act.wait_ge(act_hi, n - 2)
                    act.wait_ge(act_lo, n - 2)
                nc.scalar.activation(act_ring[:, n % 3, slot, :], up_banks(n)[0][:, 0:HT],
                                     ACT.Silu).then_inc((silu1, silu2)[slot], 1)

            def hi_parts(n):
                act.wait_ge(actw, n + 1)
                if n >= 2:
                    act.wait_ge(down_mm, n - 1)
                nc.scalar.activation(actr[n % 2][0][:], act_ring[:, n % 3, :, :].rearrange("p s t -> p (s t)"),
                                     ACT.Copy).then_inc(act_hi, 1)
                act.wait_ge(mixed, n + 1)
                nc.scalar.activation(mixr[n % 2][0][:], mix_ring[:, n % 2, :], ACT.Copy).then_inc(mix_hi, 1)

            for name in ("w_a", "x0_a", "w_b", "x0_b", "x1", "valout", "small"):
                hi_part(name)
            act.wait_ge(vo_mm, 1)
            nc.scalar.activation(vo[0][:], bank[0][:, :], ACT.Copy).then_inc(vo_hi, 1)
            xT_hi_part(0)
            hi_part("ffn0")
            v_hi_part(0)
            act.wait_ge(s_pads, 1)
            qk_hi_part(0)
            xT_hi_part(1)
            exp_scores(0)
            v_hi_part(1)
            qk_hi_part(1)
            pT_hi_part(0)
            exp_scores(1)
            hi_part("ffn1")
            pT_hi_part(1)
            hi_part("ffn2")
            for h in range(HALVES):
                xT_hi_part(2 + h)
                act.wait_ge(gate_mm, h + 1)
                act.wait_ge(logits_ready, h + 1)
                for w in range(2):
                    nc.scalar.activation(ranks[h][:, w, :], rank_bank(h, w)[:, 0:HT], ACT.Copy).then_inc(ranks_ready, 1)
                act.wait_ge(gap_ready, h + 1)
                nc.scalar.activation(gap_exp[:], gap[:], ACT.Exp).then_inc(gap_exp_ready, 1)
            hi_part("ffn3")
            for h in range(HALVES):
                expand(h)
                for t in range(FT + 1):
                    n = h * FT + t
                    if t < FT:
                        silu(n, 0)
                    if t >= 1:
                        silu(n - 1, 1)
                        hi_parts(n - 1)
                act.wait_ge(low_ready, h + 1)
                nc.scalar.activation(lowr[0][:], low_sum[:], ACT.Copy).then_inc(low_hi, 1)
                act.wait_ge(y_mm, h + 1)
                if h:
                    act.wait_ge(s_out, 16 * h)
                nc.scalar.activation(yT[:, 0, :], bank[6][:, 0:HT], ACT.Copy).then_inc(y_act, 1)

        @block.vector
        def _(dve):
            chain = [0]

            def link(ins):
                chain[0] += 1
                ins.then_inc(s_chain, 1)
                dve.wait_ge(s_chain, chain[0])

            def lo_part(name):
                dve.wait_ge(hi_done[name], 1)
                slot, _src, (hi, lo) = load_at[name]
                nc.vector.tensor_tensor(lo, slot, as_f32(hi), ALU.subtract).then_inc(lo_done[name], 1)

            def moments_of(h, n):
                for g in range(GROUPS):
                    nc.vector.bn_stats(stats[:, g, :], resid[h][:, g, :]).then_inc(s_chain, 1)
                chain[0] += GROUPS
                dve.wait_ge(s_chain, chain[0])
                for g in range(GROUPS):
                    nc.vector.bn_aggr(moments[:, g, :], stats[:, g, :]).then_inc(moments_ready, 1)

            def normalise(h, n):
                dve.wait_ge(rstd_ready, n + 1)
                if n:
                    dve.wait_ge(xT_mm, n)
                for g in range(GROUPS):
                    last = nc.vector.tensor_scalar(xnorm[:, g, :], resid[h][:, g, :], moments[:, g, 0:1],
                                                   rstd[:, g:g + 1], ALU.subtract, ALU.mult)
                last.then_inc(xnorm_ready, 1)

            def embed_rows(h):
                for g in range(GROUPS):
                    dve.wait_ge(tok_done, GROUPS * h + g + 1)
                    nc.vector.tensor_tensor(resid[h][:, g, :], bank[1 + 3 * h + g][0:GR, 0:D], add_rows[:],
                                            ALU.add).then_inc(resid_ready, 1)
                dve.wait_ge(resid_ready, GROUPS * (h + 1))

            def xT_lo_part(n):
                for k in range(KD):
                    dve.wait_ge(xT_hi, KD * n + k + 1)
                    at = slice(k * HPE, k * HPE + HP)
                    nc.vector.tensor_tensor(xT[n % 2][1][:, at], xT_bank(n, k)[:, 0:HP],
                                            as_f32(xT[n % 2][0][:, at]), ALU.subtract).then_inc(xT_lo, 1)

            def rotate(h):
                dve.wait_ge(qk_mm, h + 1)
                even, odd = rope_banks[:, 0:2, 0:HT], rope_banks[:, 2:4, 0:HT]
                for i, (half, at) in enumerate(((even, C_COS), (odd, C_SIN), (even, C_SIN), (odd, C_COS))):
                    if h and i == 0:
                        dve.wait_ge(qk_hi, 2 * h)
                        dve.wait_ge(qk_lo, 2 * h)
                        dve.wait_ge(rot_odd, h)
                    factor = cst[:, at:at + ROWS].unsqueeze(1).to_broadcast([P, HALF_IMAGES, ROWS])
                    for s in range(2):
                        nc.vector.tensor_tensor(rot[i][:, s, :].rearrange("p (b t) -> p b t", t=ROWS),
                                                half[:, s, :].rearrange("p (b t) -> p b t", t=ROWS),
                                                factor, ALU.mult).then_inc(rot_read, 1)
                dve.wait_ge(rot_read, 8 * (h + 1))
                nc.vector.tensor_tensor(rot[0][:], rot[0][:], rot[1][:], ALU.subtract).then_inc(rot_even, 1)
                nc.vector.tensor_tensor(rot[2][:], rot[2][:], rot[3][:], ALU.add).then_inc(rot_odd, 1)

            def qk_lo_part(h):
                for i in range(2):
                    dve.wait_ge(qk_hi, 2 * h + i + 1)
                    lo, hi = (part[:].rearrange("p (i t) -> p i t", i=4)[:, 2 * i:2 * i + 2, 0:HT]
                              for part in (qk[1], qk[0]))
                    nc.vector.tensor_tensor(lo, rot[2 * i][:], as_f32(hi), ALU.subtract).then_inc(qk_lo, 1)

            def v_lo_part(h):
                dve.wait_ge(v_hi, GROUPS * (h + 1))
                for g in range(GROUPS):
                    at = slice(g * D, (g + 1) * D)
                    nc.vector.tensor_tensor(val[h][1][0:GR, at], v_banks(h, g), as_f32(val[h][0][0:GR, at]),
                                            ALU.subtract).then_inc(v_lo, 1)

            def mask_scores(h):
                dve.wait_ge(s_mm, h + 1)
                if h:
                    dve.wait_ge(p_ready, GROUPS * h)
                nc.vector.tensor_tensor(scores[:], bank[1][0:GR, 0:GROUPS * GRE].rearrange("p (g t) -> p g t", t=GRE),
                                        far_mask.unsqueeze(1).to_broadcast([GR, GROUPS, GRE]),
                                        ALU.add).then_inc(s_masked, 1)
                dve.wait_ge(s_masked, h + 1)
                link(nc.vector.tensor_reduce(top[:], scores[:], AX_X, ALU.max))
                nc.vector.tensor_scalar(neg_top[:], top[:], -SCORE_SCALE, None, ALU.mult).then_inc(s_negtop, 1)

            def inv_sums(h):
                dve.wait_ge(p_ready, GROUPS * (h + 1))
                if h:
                    dve.wait_ge(h2_ready, GROUPS * h)
                nc.vector.reciprocal(inv_total[:], total[:]).then_inc(inv_ready, 1)

            def pT_lo_part(h):
                dve.wait_ge(pT_hi, h + 1)
                nc.vector.tensor_tensor(probsT[1][0:GR, :], bank[2][0:GR, 0:HP], as_f32(probsT[0][0:GR, :]),
                                        ALU.subtract).then_inc(pT_lo, 1)

            def add_attention(h):
                dve.wait_ge(pv_mm, h + 1)
                dve.wait_ge(inv_ready, h + 1)
                for g in range(GROUPS):
                    nc.vector.scalar_tensor_tensor(out=resid[h][:, g, :], in0=v_banks(h, g),
                                                   scalar=inv_total[:, g:g + 1], in1=resid[h][:, g, :],
                                                   op0=ALU.mult, op1=ALU.add).then_inc(h2_ready, 1)
                dve.wait_ge(h2_ready, GROUPS * (h + 1))

            def choose(h):
                dve.wait_ge(gate_mm, h + 1)
                src = rank_bank(h, 1)[0:GR, HT:HT + GROUPS * EXPERTS].rearrange("p (g e) -> p g e", e=EXPERTS)
                nc.vector.tensor_copy(logits[:], src).then_inc(logits_ready, 1)
                dve.wait_ge(logits_ready, h + 1)
                order = cst[0:GR, C_RANK:C_RANK + EXPERTS].unsqueeze(1).to_broadcast([GR, GROUPS, EXPERTS])
                for s, lg in enumerate((logits, logits2)):
                    wide = lambda x: x.unsqueeze(2).to_broadcast([GR, GROUPS, EXPERTS])
                    link(nc.vector.tensor_reduce(best[:, s, :], lg[:], AX_X, ALU.max))
                    link(nc.vector.tensor_tensor(hits[:], lg[:], wide(best[:, s, :]), ALU.is_equal))
                    link(nc.vector.tensor_tensor(hits[:], hits[:], order, ALU.mult))
                    link(nc.vector.tensor_reduce(first[:], hits[:], AX_X, ALU.max))
                    link(nc.vector.tensor_tensor(chosen[s][:], hits[:], wide(first[:]), ALU.is_equal))
                    if s == 0:
                        link(nc.vector.scalar_tensor_tensor(out=logits2[:], in0=chosen[0][:], scalar=TAKEN,
                                                            in1=logits[:], op0=ALU.mult, op1=ALU.add))
                nc.vector.tensor_tensor(gap[:], best[:, 1, :], best[:, 0, :], ALU.subtract).then_inc(gap_ready, 1)
                if h:
                    dve.wait_ge(expand_mm, h)
                for s in range(2):
                    src = chosen[s][:].unsqueeze(3).to_broadcast([GR, GROUPS, EXPERTS, RANK])
                    link(nc.vector.tensor_scalar(chosen_x[:, s], src, LORA_SCALE, None, ALU.mult))
                dve.wait_ge(gap_exp_ready, h + 1)
                link(nc.vector.tensor_scalar(gap_den[:], gap_exp[:], 1.0, None, ALU.add))
                link(nc.vector.reciprocal(slot_w[:, 0, :], gap_den[:]))
                link(nc.vector.tensor_tensor(slot_w[:, 1, :], gap_exp[:], slot_w[:, 0, :], ALU.mult))
                nc.vector.tensor_copy(slot_wx[:], slot_w[:].unsqueeze(3).to_broadcast([GR, 2, GROUPS, P])).then_inc(slots_ready, 1)

            def slot_inputs(h):
                dve.wait_ge(mask_ready, 2 * (h + 1))
                dve.wait_ge(ranks_ready, 2 * (h + 1))
                if h:
                    dve.wait_ge(slot_hi, h)
                for s in range(2):
                    nc.vector.tensor_tensor(slot_in[:, s, :, :], ranks[h][:],
                                            mask[:, s, :].unsqueeze(1).to_broadcast([P, 2, HT]), ALU.mult).then_inc(slot_in_ready, 1)
                dve.wait_ge(slot_in_ready, 3 * h + 2)
                nc.vector.tensor_tensor(slot_in[:, 1, :, :], slot_in[:, 1, :, :], slot_in[:, 0, :, :],
                                        ALU.subtract).then_inc(slot_in_ready, 1)
                dve.wait_ge(slot_hi, h + 1)
                nc.vector.tensor_tensor(slot_inr[1][:], slot_in[:].rearrange("p s w t -> p (s w t)"),
                                        as_f32(slot_inr[0][:]), ALU.subtract).then_inc(slot_lo, 1)

            def gated(n, slot):
                dve.wait_ge((silu1, silu2)[slot], n + 1)
                at = act_ring[:, n % 3, slot, :]
                nc.vector.tensor_tensor(at, up_banks(n)[1][:, 0:HT], at, ALU.mult).then_inc((act1, act2)[slot], 1)

            def weighted(n):
                dve.wait_ge(act1, n + 1)
                dve.wait_ge(act2, n + 1)
                dve.wait_ge(weight_ready, 2 * (n // FT + 1))
                at = act_ring[:, n % 3, :, :]
                nc.vector.tensor_tensor(at, at, weight[:], ALU.mult).then_inc(actw, 1)

            def lo_parts(n):
                if n >= 2:
                    dve.wait_ge(down_mm, n - 1)
                dve.wait_ge(act_hi, n + 1)
                nc.vector.tensor_tensor(actr[n % 2][1][:], act_ring[:, n % 3, :, :].rearrange("p s t -> p (s t)"),
                                        as_f32(actr[n % 2][0][:]), ALU.subtract).then_inc(act_lo, 1)
                dve.wait_ge(mix_hi, n + 1)
                nc.vector.tensor_tensor(mixr[n % 2][1][:], mix_ring[:, n % 2, :], as_f32(mixr[n % 2][0][:]),
                                        ALU.subtract).then_inc(mix_lo, 1)

            for name in ("w_a", "x0_a", "w_b", "x0_b"):
                lo_part(name)
            dve.wait_ge(s_table, 16)
            dve.wait_ge(s_const, 16)
            nc.vector.tensor_tensor(add_rows[:], tab[:, 0, :], tab[:, 1, :], ALU.add).then_inc(s_rows, 1)
            nc.vector.tensor_copy(ident_bf[:], ident).then_inc(s_ident, 1)
            dve.wait_ge(s_rows, 1)
            lo_part("x1")
            embed_rows(0)
            moments_of(0, 0)
            lo_part("valout")
            normalise(0, 0)
            lo_part("small")
            embed_rows(1)
            moments_of(1, 1)
            dve.wait_ge(vo_hi, 1)
            nc.vector.tensor_tensor(vo[1][:], bank[0][:, :], as_f32(vo[0][:]), ALU.subtract).then_inc(vo_lo, 1)
            xT_lo_part(0)
            normalise(1, 1)
            rotate(0)
            v_lo_part(0)
            qk_lo_part(0)
            xT_lo_part(1)
            mask_scores(0)
            rotate(1)
            inv_sums(0)
            v_lo_part(1)
            qk_lo_part(1)
            pT_lo_part(0)
            mask_scores(1)
            add_attention(0)
            moments_of(0, 2)
            inv_sums(1)
            normalise(0, 2)
            pT_lo_part(1)
            xT_lo_part(2)
            add_attention(1)
            moments_of(1, 3)
            choose(0)
            normalise(1, 3)
            xT_lo_part(3)
            choose(1)
            for h in range(HALVES):
                slot_inputs(h)
                for t in range(FT + 1):
                    n = h * FT + t
                    if t < FT:
                        gated(n, 0)
                    if t >= 1:
                        gated(n - 1, 1)
                        weighted(n - 1)
                        lo_parts(n - 1)
                dve.wait_ge(down_mm, FT * (h + 1))
                for s in range(2):
                    nc.vector.tensor_tensor(low[:, s, :], bank[4 + s][:, 0:HT], mask[:, s, :],
                                            ALU.mult).then_inc(s_chain, 1)
                chain[0] += 2
                dve.wait_ge(s_chain, chain[0])
                if h:
                    dve.wait_ge(low_lo, h)
                nc.vector.tensor_tensor(low_sum[:], low[:, 0, :], low[:, 1, :], ALU.add).then_inc(low_ready, 1)
                dve.wait_ge(low_hi, h + 1)
                nc.vector.tensor_tensor(lowr[1][:], low_sum[:], as_f32(lowr[0][:]), ALU.subtract).then_inc(low_lo, 1)
                dve.wait_ge(y_mm, h + 1)
                if h:
                    dve.wait_ge(s_out, 16 * h)
                nc.vector.tensor_copy(yT[:, 1, :], bank[7][:, 0:HT]).then_inc(y_dve, 1)

        @block.tensor
        def _(pe):
            def product(dst, w, x, start, stop, open_bank=False):
                nc.tensor.matmul(dst, w[0], x[0], start=start, stop=False, skip_group_check=open_bank)
                nc.tensor.matmul(dst, w[0], x[1], start=False, stop=False, skip_group_check=open_bank)
                return nc.tensor.matmul(dst, w[1], x[0], start=False, stop=stop, skip_group_check=open_bank)

            def cols(parts, a, b, rows=P):
                return [p[0:rows, a:b] for p in parts]

            def split(name):
                pe.wait_ge(hi_done[name], 1)
                pe.wait_ge(lo_done[name], 1)

            def embedding(h):
                for k in range(KX):
                    if k == 0:
                        split("x0_a" if h == 0 else "x1")
                        split("w_a")
                    if k == KX // 2 and h == 0:
                        split("x0_b")
                        split("w_b")
                    for g in range(GROUPS):
                        at = k * HP + g * GR
                        last = product(bank[1 + 3 * h + g][0:GR, 0:D], cols(xhalf[h], at, at + GR),
                                       cols(embed, k * D, (k + 1) * D), k == 0, k == KX - 1)
                        if k == KX - 1:
                            last.then_inc(tok_done, 1)

            def value_out():
                split("valout")
                for m in range(KD):
                    for k in range(KD):
                        last = product(bank[0][:, m * D:(m + 1) * D], cols(valout, k * D + m * P, k * D + (m + 1) * P),
                                       cols(valout, (KD + k) * D, (KD + k + 1) * D), k == 0, k == KD - 1)
                last.then_inc(vo_mm, 1)

            def transpose_rows(n):
                pe.wait_ge(xnorm_ready, n + 1)
                pe.wait_ge(s_const, 16)
                if n == 0:
                    pe.wait_ge(resid_ready, 2)
                elif n == 1:
                    pe.wait_ge(xT_lo, KD)
                elif n == 2:
                    pe.wait_ge(rot_read, 2 * 8)
                else:
                    pe.wait_ge(xT_lo, 3 * KD)
                for k in range(KD):
                    for g in range(GROUPS):
                        last = nc.tensor.transpose(xT_bank(n, k)[:, g * GR:(g + 1) * GR],
                                                   xnorm[:, g, k * P:(k + 1) * P], ident[0:GR, 0:GR])
                last.then_inc(xT_mm, 1)

            def queries_keys(h):
                split("small")
                pe.wait_ge(xT_lo, KD * (h + 1))
                if h == 0:
                    pe.wait_ge(resid_ready, 2 * GROUPS)
                else:
                    pe.wait_ge(rot_read, 8 * h)
                for m in range(4):
                    for k in range(KD):
                        at = M_QK + (k * 4 + m) * P
                        last = product(rope_banks[:, m, 0:HT], cols(small, at, at + P),
                                       cols(xT[h], k * HPE, k * HPE + HT), k == 0, k == KD - 1)
                last.then_inc(qk_mm, 1)

            def values(h):
                pe.wait_ge(vo_lo, 1)
                if h == 0:
                    pe.wait_ge(resid_ready, GROUPS)
                else:
                    pe.wait_ge(rot_read, 2 * 8)
                for g in range(GROUPS):
                    for k in range(KD):
                        at = k * HPE + g * GR
                        last = product(v_banks(h, g), cols(xT[h], at, at + GR), cols(vo, k * D, (k + 1) * D),
                                       k == 0, k == KD - 1)
                last.then_inc(v_mm, 1)

            def score(h):
                pe.wait_ge(qk_lo, 2 * (h + 1))
                pe.wait_ge(s_pads, 1)
                if h == 0:
                    pe.wait_ge(xT_lo, 2 * KD)
                else:
                    pe.wait_ge(s_masked, h)
                for g in range(GROUPS):
                    for k in range(KD):
                        q, key = 2 * k * HPE + g * GR, (2 * k + 1) * HPE + g * GR
                        last = product(bank[1][0:GR, g * GRE:(g + 1) * GRE], cols(qk, q, q + GR),
                                       cols(qk, key, key + GRE), k == 0, k == KD - 1)
                last.then_inc(s_mm, 1)

            def transpose_probs(h):
                pe.wait_ge(p_ready, GROUPS * (h + 1))
                if h == 0:
                    pe.wait_ge(xT_lo, 2 * KD)
                else:
                    pe.wait_ge(pT_lo, h)
                for g in range(GROUPS):
                    last = nc.tensor.transpose(bank[2][0:GR, g * GR:(g + 1) * GR], probs[:, g, 0:GR],
                                               ident[0:GR, 0:GR])
                last.then_inc(pT_mm, 1)

            def weighted_values(h):
                pe.wait_ge(pT_lo, h + 1)
                pe.wait_ge(v_lo, GROUPS * (h + 1))
                for g in range(GROUPS):
                    last = product(v_banks(h, g), cols(probsT, g * GR, (g + 1) * GR, GR),
                                   cols(val[h], g * D, (g + 1) * D, GR), True, True)
                last.then_inc(pv_mm, 1)

            def gates(h):
                pe.wait_ge(xT_lo, KD * (h + 3))
                x = xT[h]
                for w in (1, 0):
                    for k in range(KD):
                        at = M_A13 + (k * 2 + w) * P
                        last = product(rank_bank(h, w)[:, 0:HT], cols(small, at, at + P),
                                       cols(x, k * HPE, k * HPE + HT), k == 0, k == KD - 1)
                for g in range(GROUPS):
                    dst = rank_bank(h, 1)[0:GR, HT + g * EXPERTS:HT + (g + 1) * EXPERTS]
                    for k in range(KD):
                        at, gt = k * HPE + g * GR, M_GATE + k * EXPERTS
                        last = product(dst, cols(x, at, at + GR), cols(small, gt, gt + EXPERTS), k == 0, k == KD - 1)
                last.then_inc(gate_mm, 1)

            def expand(h):
                pe.wait_ge(slots_ready, h + 1)
                pe.wait_ge(s_ident, 1)
                if h == 0:
                    pe.wait_ge(ranks_ready, 2)
                else:
                    pe.wait_ge(act2, FT)
                for s in range(2):
                    for g in range(GROUPS):
                        rows = min(GR, HT - g * GR)
                        nc.tensor.matmul(bank[s][:, g * GR:g * GR + rows],
                                         chosen_x[:, s, g].rearrange("p e r -> p (e r)"), ident_bf[0:GR, 0:rows],
                                         start=True, stop=True)
                    for g in range(GROUPS):
                        rows = min(GR, HT - g * GR)
                        last = nc.tensor.matmul(bank[2 + s][:, g * GR:g * GR + rows], slot_wx[:, s, g, :],
                                                ident[0:GR, 0:rows], start=True, stop=True)
                last.then_inc(expand_mm, 1)

            def up_slot1(n):
                h, t = divmod(n, FT)
                if t == 0:
                    pe.wait_ge(slot_lo, h + 1)
                    pe.wait_ge(weight_ready, 2 * (h + 1))
                elif t >= 2:
                    pe.wait_ge(act2, n - 1)
                if h == 0 and t % CHUNK_TILES == 0:
                    split(f"ffn{t // CHUNK_TILES}")
                for w in range(2):
                    for k in range(KD):
                        at = T_UP + (w * KD + k) * P
                        product(up_banks(n)[w][:, 0:HT], [ffn_w_at(p, t, at) for p in range(2)],
                                cols(xT[h], k * HPE, k * HPE + HT), k == 0, False)
                    last = product(up_banks(n)[w][:, 0:HT], [ffn_w_at(p, t, T_B13 + w * P) for p in range(2)],
                                   cols(slot_inr, w * HT, (w + 1) * HT), False, True)
                last.then_inc(up1_mm, 1)

            def up_slot2(n):
                t = n % FT
                pe.wait_ge(act1, n + 1)
                for w in range(2):
                    last = product(up_banks(n)[w][:, 0:HT], [ffn_w_at(p, t, T_B13 + w * P) for p in range(2)],
                                   cols(slot_inr, (2 + w) * HT, (3 + w) * HT), False, True, True)
                last.then_inc(up2_mm, 1)

            def residual(h):
                if h == 0:
                    pe.wait_ge(ranks_ready, 2 * 2)
                else:
                    pe.wait_ge(y_act, h)
                    pe.wait_ge(y_dve, h)
                pe.wait_ge(h2_ready, GROUPS * (h + 1))
                for m in range(KD):
                    for g in range(GROUPS):
                        rows = min(GR, HT - g * GR)
                        nc.tensor.matmul(bank[6 + m][:, g * GR:g * GR + rows], resid[h][:, g, m * P:(m + 1) * P],
                                         ident[0:GR, 0:rows], start=(g == 0), stop=False, skip_group_check=True)

            def down(n):
                h, t = divmod(n, FT)
                if t == 0:
                    residual(h)
                    if h == 0:
                        pe.wait_ge(xT_lo, 4 * KD)
                    else:
                        pe.wait_ge(low_ready, h)
                pe.wait_ge(act_lo, n + 1)
                for s in range(2):
                    product(bank[4 + s][:, 0:HT], [ffn_w_at(p, t, T_A2) for p in range(2)],
                            cols(actr[n % 2], s * HT, (s + 1) * HT), t == 0, t == FT - 1)
                pe.wait_ge(mix_lo, n + 1)
                for m in range(KD):
                    last = product(bank[6 + m][:, 0:HT], [ffn_w_at(p, t, T_DOWN + m * P) for p in range(2)],
                                   cols(mixr[n % 2], 0, HT), False, False, True)
                last.then_inc(down_mm, 1)

            def low_out(h):
                pe.wait_ge(low_lo, h + 1)
                for m in range(KD):
                    at = M_B2 + m * P
                    last = product(bank[6 + m][:, 0:HT], cols(small, at, at + P), cols(lowr, 0, HT), False, True, True)
                last.then_inc(y_mm, 1)

            embedding(0)
            embedding(1)
            value_out()
            transpose_rows(0)
            queries_keys(0)
            values(0)
            transpose_rows(1)
            queries_keys(1)
            score(0)
            values(1)
            transpose_probs(0)
            score(1)
            weighted_values(0)
            transpose_probs(1)
            weighted_values(1)
            transpose_rows(2)
            gates(0)
            transpose_rows(3)
            gates(1)
            for h in range(HALVES):
                expand(h)
                for t in range(FT + 2):
                    n = h * FT + t
                    if t < FT:
                        up_slot1(n)
                    if 1 <= t <= FT:
                        up_slot2(n - 1)
                    if t >= 2:
                        down(n - 2)
                low_out(h)


def kernel(x, L0_tok_W, L0_tok_b, L0_tok_cls_token, L0_tok_pos_enc, L0_attn_wq, L0_attn_wk, L0_attn_wv, L0_attn_wo,
           L0_ffn_gate_w, L0_ffn_w_gate, L0_ffn_w_up, L0_ffn_w_down, L0_ffn_A1, L0_ffn_B1, L0_ffn_A3, L0_ffn_B3,
           L0_ffn_A2, L0_ffn_B2):
    import concourse.bacc as bacc
    from concourse.bass_utils import run_bass_kernel_spmd

    x = np.asarray(x)
    f32 = np.float32

    def tiles(a):
        return a.reshape(-1, P, a.shape[1]).transpose(1, 0, 2)

    def flat(a):
        return a.reshape(P, -1)

    rows = x.reshape(IMAGES, CHANNELS, GRID, PATCH, GRID, PATCH).transpose(0, 2, 4, 1, 3, 5)
    rows = rows.reshape(HALVES, HALF_IMAGES, ROWS - 1, KX * P)
    padded = np.zeros((HALVES, GROUPS * GROUP_IMAGES, ROWS, KX * P), f32)
    padded[:, :HALF_IMAGES, 1:] = rows
    patches = padded.reshape(HALVES, HP, KX, P).transpose(3, 0, 2, 1).reshape(P, HALVES, KX * HP)

    embed_w = flat(tiles(np.asarray(L0_tok_W).T))
    wv, wo = np.asarray(L0_attn_wv), np.asarray(L0_attn_wo)
    value_w = np.concatenate([flat(tiles(wv)), flat(tiles(wo.T))], axis=1)
    qT, kT = np.asarray(L0_attn_wq).T, np.asarray(L0_attn_wk).T
    qk = np.stack([qT[:, 0::2], kT[:, 0::2], qT[:, 1::2], kT[:, 1::2]], axis=1).reshape(D, 4 * P)
    ranks_first = lambda a: np.asarray(a).reshape(EXPERTS * RANK, -1).T
    a13 = np.concatenate([ranks_first(L0_ffn_A1), ranks_first(L0_ffn_A3)], axis=1)
    by_rank = lambda b: np.asarray(b).transpose(0, 2, 1).reshape(EXPERTS * RANK, -1)
    small_w = np.concatenate([flat(tiles(qk)), flat(tiles(a13)), flat(tiles(np.asarray(L0_ffn_gate_w).T)),
                              by_rank(L0_ffn_B2)], axis=1)
    up = np.stack([np.asarray(L0_ffn_w_gate).T, np.asarray(L0_ffn_w_up).T])
    up = up.reshape(2, KD, P, FT, P).transpose(2, 3, 0, 1, 4).reshape(P, FT, -1)
    b13 = np.stack([by_rank(L0_ffn_B1), by_rank(L0_ffn_B3)]).reshape(2, P, FT, P).transpose(1, 2, 0, 3).reshape(P, FT, -1)
    a2 = tiles(ranks_first(L0_ffn_A2))
    dn = tiles(np.asarray(L0_ffn_w_down).T)
    ffn_w = np.concatenate([up, b13, a2, dn], axis=2).reshape(P, CHUNKS, STAGE)

    pos = np.tile(np.asarray(L0_tok_pos_enc)[0], (GROUP_IMAGES, 1))
    image = np.tile(np.asarray(L0_tok_b)[None, :], (ROWS, 1))
    image[0] = np.asarray(L0_tok_cls_token)[0, 0]
    table = np.stack([pos, np.tile(image, (GROUP_IMAGES, 1))], axis=1)

    const = np.zeros((P, C_ALL), f32)
    const[:, C_ID:C_ID + P] = np.eye(P, dtype=f32)
    i, j = np.arange(P)[:, None] // ROWS, np.arange(GRE)[None, :] // ROWS
    const[:, C_MASK:C_MASK + GRE] = np.where(i == j, 0.0, FAR)
    inv = (f32(1.0) / f32(10000.0) ** (np.arange(0, D, 2, dtype=f32) / f32(D))).astype(f32)
    angle = np.outer(inv, np.arange(ROWS, dtype=f32)).astype(f32)
    const[:, C_COS:C_COS + ROWS] = np.cos(angle)
    const[:, C_SIN:C_SIN + ROWS] = np.sin(angle)
    const[:, C_RANK:] = np.arange(EXPERTS, 0, -1)

    arrays = {"patches": patches, "embed_w": embed_w, "value_w": value_w, "small_w": small_w, "ffn_w": ffn_w,
              "const": const, "table": table}
    arrays = {k: np.ascontiguousarray(v) for k, v in arrays.items()}
    nc = bacc.Bacc("TRN2", target_bir_lowering=False, num_devices=1)
    args = [nc.dram_tensor(k, v.shape, F32, kind="ExternalInput").ap() for k, v in arrays.items()]
    out = nc.dram_tensor("out", (P, HALVES, KD, HT), F32, kind="ExternalOutput").ap()
    vit_block(nc, *args, out)
    r = run_bass_kernel_spmd(nc, [arrays], core_ids=[0])
    got = r.results[0]["out"]
    return np.ascontiguousarray(got.transpose(1, 3, 2, 0).reshape(IMAGES, ROWS, D))
```

```python
from contextlib import ExitStack

import numpy as np
import concourse.bass as bass
from concourse import mybir

ALU = mybir.AluOpType
ACT = mybir.ActivationFunctionType
AX_X = mybir.AxisListType.X
F32 = mybir.dt.float32
F32R = mybir.dt.float32r
BF16 = mybir.dt.bfloat16

P = 128
IMAGES, CHANNELS, SIDE, PATCH = 16, 3, 96, 16
D = 256
F = 1024
EXPERTS, RANK = 8, 16
GRID = SIDE // PATCH
ROWS = GRID * GRID + 1
HALVES = 2
HALF_IMAGES = IMAGES // HALVES
GROUP_IMAGES = 3
GROUPS = -(-HALF_IMAGES // GROUP_IMAGES)
GR = GROUP_IMAGES * ROWS
GRE = GR + 1
HT = HALF_IMAGES * ROWS
HP = GROUPS * GR
HPE = HP + 1
KX = CHANNELS * PATCH * PATCH // P
KD = D // P
FT = F // P
EPS = 1e-5
SCORE_SCALE = float(D) ** -0.5
LORA_SCALE = 2.0
FAR = -1e30
LEAST = 1.1754944e-38

C_ID, C_MASK = 0, P
C_COS = C_MASK + GRE
C_SIN = C_COS + ROWS
C_ORDER = C_SIN + ROWS
C_ALL = C_ORDER + EXPERTS * EXPERTS
M_QK = 0
M_A13 = M_QK + KD * 4 * P
M_GATE = M_A13 + KD * 2 * P
M_B2 = M_GATE + KD * EXPERTS
M_ALL = M_B2 + KD * P
T_UP = 0
T_B13 = T_UP + 2 * KD * P
T_A2 = T_B13 + 2 * P
T_DOWN = T_A2 + P
T_ALL = T_DOWN + KD * P
NS = HALVES * FT
UP_PAIRS_FROM = FT + 3
STAGES = 5
STAGE = T_ALL


def vit_block(nc, patches, embed_w, value_w, small_w, ffn_w, const, table, out):
    ctx = ExitStack()
    with ctx:
        def sb(name, shape, dt=F32, where=ctx):
            return where.enter_context(nc.sbuf_tensor(name, shape, dt))

        def pair(name, cols, where=ctx):
            return [sb(f"{name}_{part}", [P, cols], F32R, where) for part in ("hi", "lo")]

        def sem(name):
            return ctx.enter_context(nc.semaphore(name))

        def as_f32(ap):
            return ap.bitcast(F32)

        cst = sb("cst", [P, C_ALL])
        table_sb = sb("table_sb", [GR, 2, D])
        ident_bf = sb("ident_bf", [P, P], BF16)
        stage = [sb(f"stage{i}", [P, STAGE]) for i in range(STAGES)]
        small = pair("small", M_ALL)
        vo = pair("vo", KD * D)
        resid = [sb(f"resid{h}", [GR, GROUPS, D]) for h in range(HALVES)]
        xnorm = sb("xnorm", [GR, GROUPS, D])
        xT = [pair(f"xT{h}", KD * HPE) for h in range(HALVES)]
        stats = sb("stats", [GR, GROUPS, 6])
        moments = sb("moments", [GR, GROUPS, 2])
        spread = sb("spread", [GR, GROUPS])
        minus_half = sb("minus_half", [GR, GROUPS])
        rstd = sb("rstd", [GR, GROUPS])
        rot = [[sb(f"rot{s}_{i}", [P, HT]) for i in range(4)] for s in range(2)]
        val = pair("val", GROUPS * D)
        top = sb("top", [GR, GROUPS])
        neg_top = sb("neg_top", [GR, GROUPS])
        total = sb("total", [GR, GROUPS])
        inv_total = sb("inv_total", [GR, GROUPS])
        logits = sb("logits", [GR, GROUPS, EXPERTS])
        versus = sb("versus", [GR, GROUPS, EXPERTS, EXPERTS])
        place = sb("place", [GR, GROUPS, EXPERTS])
        second = sb("second", [GR, GROUPS, EXPERTS])
        best = sb("best", [GR, 2, GROUPS])
        gap = sb("gap", [GR, GROUPS])
        gap_tanh = sb("gap_tanh", [GR, GROUPS])
        slot_w = sb("slot_w", [GR, 2, GROUPS])
        slot_wx = sb("slot_wx", [GR, 2, GROUPS, P])
        chosen_x = sb("chosen_x", [GR, 2, GROUPS, EXPERTS, RANK], BF16)
        ranks = sb("ranks", [P, 2, HT])
        mask = [sb(f"mask{h}", [P, 2, HT]) for h in range(HALVES)]
        weight = sb("weight", [P, 2, HT])
        slot_in = sb("slot_in", [P, 2, 2, HT])
        slot_inr = pair("slot_inr", 4 * HT)
        act_ring = sb("act_ring", [P, 2, 2, HT])
        actr = [pair(f"actr{i}", 2 * HT) for i in range(2)]
        mix_ring = sb("mix_ring", [P, 2, HT])
        mixr = [pair(f"mixr{i}", HT) for i in range(2)]
        lowr = pair("lowr", HT)
        low, low_sum, yT = slot_in[:, 0], slot_in[:, 1, 0], slot_in[:, 0]
        with ExitStack() as early:
            xhalf = [pair("xhalf0", KX * HP, early)]
        with ExitStack() as attn:
            qk = pair("qk", 4 * HPE, attn)
            scores = sb("scores", [GR, GROUPS, GRE], F32, attn)
            probsT = pair("probsT", HP, attn)
        over = max(2 * KX * HP, 2 * 4 * HPE + GROUPS * GRE + 2 * HP)
        sb("overlaid", [P, over])
        ffn = [pair(f"ffn{t}", T_ALL) for t in range(FT // 2)]
        with ExitStack() as early:
            xhalf.append(pair("xhalf1", KX * HP, early))
            embed = pair("embed", KX * D, early)
            valout = pair("valout", 2 * KD * D, early)
        ffn += [pair(f"ffn{t}", T_ALL) for t in range(FT // 2, FT)]

        bank = [ctx.enter_context(nc.psum_tensor(f"bank{i}", [P, 512], F32)) for i in range(8)]

        third_x, third_w = KX // 3 * HP, KX // 3 * D

        def part_of(parts, a, b):
            return [p[:, a:b] for p in parts]

        def embed_load(i):
            at = (i * third_w, (i + 1) * third_w)
            return (f"w{i}", embed_w[:, at[0]:at[1]], part_of(embed, *at))

        def patch_load(h, i):
            at = (i * third_x, (i + 1) * third_x)
            return (f"x{h}_{i}", patches[:, h, at[0]:at[1]], part_of(xhalf[h], *at))

        LOADS = [load for i in range(3) for load in (embed_load(i), patch_load(0, i))]
        LOADS += [("valout", value_w, part_of(valout, 0, 2 * KD * D))]
        LOADS += [patch_load(1, i) for i in range(3)]
        LOADS += [("qk_w", small_w[:, 0:M_A13], part_of(small, 0, M_A13)),
                  ("rest_w", small_w[:, M_A13:M_ALL], part_of(small, M_A13, M_ALL))]
        LOADS += [(f"ffn{t}", ffn_w[:, t, :], part_of(ffn[t], 0, T_ALL)) for t in range(FT)]
        NAMES = [name for name, *_ in LOADS]
        load_at = {name: (stage[i % STAGES][:, 0:src.shape[1]], src, parts)
                   for i, (name, src, parts) in enumerate(LOADS)}
        loaded = [sem(f"stage{i}_loaded") for i in range(STAGES)]
        hi_done = sem("staged_hi_done")
        lo_done = {name: sem(f"{name}_lo_done") for name in NAMES}

        s_const, s_table = sem("const_loaded"), sem("table_loaded")
        s_rows, s_ident, s_pads, s_mhalf = sem("table_summed"), sem("ident_bf_ready"), sem("pads_cleared"), sem("minus_half_ready")
        tok_mm, resid_ready = sem("tok_mm"), sem("resid_ready")
        vo_mm, vo_hi, vo_lo = sem("vo_mm"), sem("vo_hi_ready"), sem("vo_lo_ready")
        stats_ready, moments_ready, spread_ready = sem("stats_ready"), sem("moments_ready"), sem("spread_ready")
        rstd_ready, xnorm_ready = sem("rstd_ready"), sem("xnorm_ready")
        xT_mm, xT_hi, xT_lo = sem("xT_mm"), sem("xT_hi_ready"), sem("xT_lo_ready")
        qk_mm, rot_read, rot_ready = sem("qk_mm"), sem("rot_read"), sem("rot_ready")
        rot_ready_q = sem("rot_ready_q")
        qk_hi, qk_lo = sem("qk_hi_ready"), sem("qk_lo_ready")
        v_mm, v_hi, v_lo = sem("v_mm"), sem("v_hi_ready"), sem("v_lo_ready")
        s_mm, s_masked, s_top, s_negtop = sem("scores_mm"), sem("scores_masked"), sem("top_ready"), sem("neg_top_ready")
        p_ready, inv_ready = sem("probs_ready"), sem("inv_total_ready")
        pT_mm, pT_hi, pT_lo, pv_mm = sem("pT_mm"), sem("pT_hi_ready"), sem("pT_lo_ready"), sem("pv_mm")
        h2_ready = sem("h2_ready")
        gate_mm, ranks_mm, logits_ready = sem("gate_mm"), sem("ranks_mm"), sem("logits_ready")
        gap_ready, tanh_ready, slots_ready = sem("gap_ready"), sem("gap_tanh_ready"), sem("slots_ready")
        chosen_ready = sem("chosen_ready")
        ranks_ready = sem("ranks_ready")
        mask_mm, mask_ready = sem("mask_mm"), sem("mask_ready")
        weight_mm, weight_ready = sem("weight_mm"), sem("weight_ready")
        slot_masked, slot_in_ready, slot_hi, slot_lo = (sem("slot_masked"), sem("slot_in_ready"), sem("slot_hi_ready"),
                                                        sem("slot_lo_ready"))
        gate1_mm, up1_mm, gate2_mm, up2_mm = sem("gate1_mm"), sem("up1_mm"), sem("gate2_mm"), sem("up2_mm")
        silu1, silu2, act1, act2 = sem("silu1_done"), sem("silu2_done"), sem("act1_done"), sem("act2_done")
        actw, act_hi, act_lo = sem("act_weighted"), sem("act_hi_ready"), sem("act_lo_ready")
        mixed, mix_hi, mix_lo = sem("mixed"), sem("mix_hi_ready"), sem("mix_lo_ready")
        down_mm = sem("down_mm")
        low_masked, low_ready, low_hi, low_lo = sem("low_masked"), sem("low_ready"), sem("low_hi_ready"), sem("low_lo_ready")
        y_mm, y_act, y_dve, s_out = sem("y_mm"), sem("y_act_copied"), sem("y_dve_copied"), sem("stored")
        s_chain = sem("dve_chain")
        s_warm = sem("table_warm")

        ident = cst[:, C_ID:C_ID + P]

        def tok_psum(h, g):
            return bank[g][0:GR, 0:D] if h == 0 else bank[4 + g // 2][0:GR, (g % 2) * D:(g % 2) * D + D]

        vo_bank = bank[6]

        def up_bank(n, w):
            return bank[4 * (n % 2) * (n >= UP_PAIRS_FROM) + w]

        low_bank = bank[2:4]

        def y_bank(h, m):
            return bank[(4, 6)[h] + m]

        def xT_bank(n, k):
            return bank[(0, 4, 0, 6)[n] + k]

        def rope_bank(s, parity):
            return bank[(6, 2)[s] + parity]

        def v_bank(h, g):
            return bank[(0, 6)[h] + g // 2][0:GR, (g % 2) * D:(g % 2) * D + D]

        def score_bank(h):
            return bank[(2, 6)[h]]

        def pT_bank(h):
            return bank[(3, 7)[h]]

        def rank_bank(h, w):
            return bank[(4, 6)[h] + w]

        def mask_bank(h, s):
            return bank[(2, 6)[h] + s]

        def weight_bank(h, s):
            return bank[(4, 6)[h] + s]

        def logit_psum(h):
            return rank_bank(h, 1)[0:GR, HT:HT + GROUPS * EXPERTS]

        def group_rows(g):
            return min(GR, HT - g * GR)

        block = ctx.enter_context(nc.Block())

        @block.sync
        def _(sp):
            for i, name in enumerate(NAMES):
                if i >= STAGES:
                    sp.wait_ge(hi_done, i - STAGES + 1)
                    sp.wait_ge(lo_done[NAMES[i - STAGES]], 1)
                slot, src, _parts = load_at[name]
                sp.dma_start(slot, src).then_inc(loaded[i % STAGES], 16)
            for h in range(HALVES):
                sp.wait_ge(y_act, h + 1)
                sp.wait_ge(y_dve, h + 1)
                sp.dma_start(out[:, h, :, :], yT).then_inc(s_out, 16)
            sp.wait_ge(s_out, 16 * HALVES)

        @block.gpsimd
        def _(pool):
            def inv_std(n):
                pool.wait_ge(moments_ready, GROUPS * (n + 1))
                nc.gpsimd.tensor_scalar(spread[:], moments[:, :, 1], EPS, None, ALU.add).then_inc(spread_ready, 1)
                pool.wait_ge(spread_ready, n + 1)
                nc.gpsimd.tensor_tensor(rstd[:], spread[:], minus_half[:], ALU.pow).then_inc(rstd_ready, 1)

            def lo_part(name):
                pool.wait_ge(hi_done, NAMES.index(name) + 1)
                slot, _src, (hi, lo) = load_at[name]
                nc.gpsimd.tensor_tensor(lo, slot, as_f32(hi), ALU.subtract).then_inc(lo_done[name], 1)

            def rotated_queries(h):
                pool.wait_ge(rot_read, 8 * h + 4)
                nc.gpsimd.tensor_tensor(rot[0][0][:], rot[0][0][:], rot[0][1][:], ALU.subtract).then_inc(rot_ready_q, 1)
                nc.gpsimd.tensor_tensor(rot[0][2][:], rot[0][2][:], rot[0][3][:], ALU.add).then_inc(rot_ready_q, 1)

            def mix(n):
                pool.wait_ge(act1, n + 1)
                pool.wait_ge(act2, n + 1)
                pool.wait_ge(weight_ready, 2 * (n // FT + 1))
                at = act_ring[:, n % 2, :, :]
                nc.gpsimd.tensor_tensor(at, at, weight[:], ALU.mult).then_inc(actw, 1)
                pool.wait_ge(actw, n + 1)
                if n >= 2:
                    pool.wait_ge(mix_hi, n - 1)
                    pool.wait_ge(mix_lo, n - 1)
                nc.gpsimd.tensor_tensor(mix_ring[:, n % 2, :], act_ring[:, n % 2, 0, :],
                                        act_ring[:, n % 2, 1, :], ALU.add).then_inc(mixed, 1)

            nc.gpsimd.memset(minus_half[:], -0.5).then_inc(s_mhalf, 1)
            pool.wait_ge(s_mhalf, 1)
            for i in range(3):
                lo_part(f"w{i}")
            lo_part("valout")
            pool.wait_ge(tok_mm, GROUPS)
            for i in range(4):
                for part in qk:
                    last = nc.gpsimd.memset(as_f32(part[:, i * HPE + HT:(i + 1) * HPE]), 0.0)
            last.then_inc(s_pads, 1)
            inv_std(0)
            lo_part("qk_w")
            lo_part("rest_w")
            rotated_queries(0)
            lo_part("ffn0")
            lo_part("ffn1")
            inv_std(1)
            lo_part("ffn2")
            inv_std(2)
            lo_part("ffn3")
            rotated_queries(1)
            for t in range(4, FT):
                lo_part(f"ffn{t}")
            for n in range(NS):
                mix(n)
                if n == 0:
                    inv_std(3)

        @block.scalar
        def _(act):
            act.dma_start(table_sb[:], table).then_inc(s_table, 16)
            act.dma_start(cst[:], const).then_inc(s_const, 16)
            act.wait_ge(s_mhalf, 1)
            nc.scalar.activation(neg_top[:], minus_half[:], ACT.Exp).then_inc(s_warm, 1)

            def hi_part(name):
                i = NAMES.index(name)
                act.wait_ge(loaded[i % STAGES], 16 * (i // STAGES + 1))
                slot, _src, (hi, _lo) = load_at[name]
                nc.scalar.activation(hi, slot, ACT.Copy).then_inc(hi_done, 1)

            def xT_hi_part(n):
                act.wait_ge(xT_mm, n + 1)
                for k in range(KD):
                    nc.scalar.activation(xT[n % 2][0][:, k * HPE:k * HPE + HP], xT_bank(n, k)[:, 0:HP],
                                         ACT.Copy).then_inc(xT_hi, 1)

            def v_hi_part(h):
                act.wait_ge(v_mm, h + 1)
                if h:
                    act.wait_ge(pv_mm, h)
                for g in range(GROUPS):
                    nc.scalar.activation(val[0][0:GR, g * D:(g + 1) * D], v_bank(h, g), ACT.Copy).then_inc(v_hi, 1)

            def qk_hi_part(h, s):
                if h and s == 0:
                    act.wait_ge(s_mm, h)
                for parity in range(2):
                    if s == 0:
                        act.wait_ge(rot_ready_q, 2 * h + parity + 1)
                    else:
                        act.wait_ge(rot_ready, 2 * h + parity + 1)
                    at = (2 * parity + s) * HPE
                    nc.scalar.activation(qk[0][:, at:at + HT], rot[s][2 * parity][:], ACT.Copy).then_inc(qk_hi, 1)

            def exp_scores(h):
                act.wait_ge(s_negtop, h + 1)
                if h:
                    act.wait_ge(inv_ready, h)
                for g in range(GROUPS):
                    nc.scalar.activation(scores[:, g, :], scores[:, g, :], ACT.Exp, bias=neg_top[:, g:g + 1],
                                         scale=SCORE_SCALE, accum_out=total[:, g:g + 1]).then_inc(p_ready, 1)

            def pT_hi_part(h):
                act.wait_ge(pT_mm, h + 1)
                if h:
                    act.wait_ge(pv_mm, h)
                nc.scalar.activation(probsT[0][0:GR, :], pT_bank(h)[0:GR, 0:HP], ACT.Copy).then_inc(pT_hi, 1)

            def ranks_copy(h):
                act.wait_ge(ranks_mm, h + 1)
                if h:
                    act.wait_ge(slot_masked, h)
                for w in range(2):
                    nc.scalar.activation(ranks[:, w, :], rank_bank(h, w)[:, 0:HT], ACT.Copy).then_inc(ranks_ready, 1)

            def gap_to_tanh(h):
                act.wait_ge(gap_ready, h + 1)
                nc.scalar.activation(gap_tanh[:], gap[:], ACT.Tanh, scale=0.5).then_inc(tanh_ready, 1)

            def mask_copy(h):
                act.wait_ge(mask_mm, h + 1)
                for s in range(2):
                    nc.scalar.activation(mask[h][:, s, :], mask_bank(h, s)[:, 0:HT], ACT.Copy).then_inc(mask_ready, 1)

            def weight_copy(h):
                act.wait_ge(weight_mm, h + 1)
                if h:
                    act.wait_ge(actw, FT)
                for s in range(2):
                    nc.scalar.activation(weight[:, s, :], weight_bank(h, s)[:, 0:HT], ACT.Copy).then_inc(weight_ready, 1)

            def slot_hi_part(h):
                if h:
                    act.wait_ge(up2_mm, FT)
                for s in range(2):
                    act.wait_ge(slot_in_ready, 2 * h + s + 1)
                    nc.scalar.activation(slot_inr[0][:, 2 * s * HT:2 * (s + 1) * HT],
                                         slot_in[:, s].rearrange("p w t -> p (w t)"), ACT.Copy).then_inc(slot_hi, 1)

            def silu(n, slot):
                if slot == 0:
                    act.wait_ge(gate1_mm, n + 1)
                    if n >= 2:
                        act.wait_ge(mixed, n - 1)
                        act.wait_ge(act_lo, n - 1)
                else:
                    act.wait_ge(gate2_mm, n + 1)
                nc.scalar.activation(act_ring[:, n % 2, slot, :], up_bank(n, 0)[:, 0:HT],
                                     ACT.Silu).then_inc((silu1, silu2)[slot], 1)

            def hi_parts(n):
                act.wait_ge(actw, n + 1)
                if n >= 2:
                    act.wait_ge(down_mm, n - 1)
                nc.scalar.activation(actr[n % 2][0][:], act_ring[:, n % 2, :, :].rearrange("p s t -> p (s t)"),
                                     ACT.Copy).then_inc(act_hi, 1)
                act.wait_ge(mixed, n + 1)
                nc.scalar.activation(mixr[n % 2][0][:], mix_ring[:, n % 2, :], ACT.Copy).then_inc(mix_hi, 1)

            def low_hi_part(h):
                act.wait_ge(low_ready, h + 1)
                nc.scalar.activation(lowr[0][:], low_sum, ACT.Copy).then_inc(low_hi, 1)

            def y_copy(h):
                act.wait_ge(y_mm, h + 1)
                nc.scalar.activation(yT[:, 0, :], y_bank(h, 0)[:, 0:HT], ACT.Copy).then_inc(y_act, 1)

            for name in NAMES[:NAMES.index("x1_0")]:
                hi_part(name)
            act.wait_ge(vo_mm, 1)
            nc.scalar.activation(vo[0][:], vo_bank[:, :], ACT.Copy).then_inc(vo_hi, 1)
            for i in range(3):
                hi_part(f"x1_{i}")
            hi_part("qk_w")
            xT_hi_part(0)
            hi_part("rest_w")
            hi_part("ffn0")
            act.wait_ge(s_pads, 1)
            qk_hi_part(0, 0)
            qk_hi_part(0, 1)
            v_hi_part(0)
            hi_part("ffn1")
            hi_part("ffn2")
            exp_scores(0)
            pT_hi_part(0)
            hi_part("ffn3")
            xT_hi_part(1)
            hi_part("ffn4")
            hi_part("ffn5")
            xT_hi_part(2)
            ranks_copy(0)
            gap_to_tanh(0)
            mask_copy(0)
            qk_hi_part(1, 0)
            slot_hi_part(0)
            qk_hi_part(1, 1)
            v_hi_part(1)
            weight_copy(0)
            hi_part("ffn6")
            hi_part("ffn7")
            exp_scores(1)
            for n in range(NS + 1):
                if n == FT:
                    slot_hi_part(1)
                if n < NS:
                    silu(n, 0)
                if n >= 1:
                    hi_parts(n - 1)
                if n == FT:
                    weight_copy(1)
                if n < NS:
                    silu(n, 1)
                if n == 0:
                    pT_hi_part(1)
                elif n == 3:
                    xT_hi_part(3)
                elif n == 5:
                    gap_to_tanh(1)
                    ranks_copy(1)
                    mask_copy(1)
                elif n == FT + 1:
                    low_hi_part(0)
                elif n == FT + 2:
                    y_copy(0)
            low_hi_part(1)
            y_copy(1)

        @block.vector
        def _(dve):
            chain = [0]

            def link(ins):
                chain[0] += 1
                ins.then_inc(s_chain, 1)
                dve.wait_ge(s_chain, chain[0])

            def lo_part(name):
                dve.wait_ge(hi_done, NAMES.index(name) + 1)
                slot, _src, (hi, lo) = load_at[name]
                nc.vector.tensor_tensor(lo, slot, as_f32(hi), ALU.subtract).then_inc(lo_done[name], 1)

            def stats_of(h, g):
                nc.vector.bn_stats(stats[:, g, :], resid[h][:, g, :]).then_inc(stats_ready, 1)

            def moments_of(n):
                if n:
                    dve.wait_ge(xnorm_ready, n)
                for g in range(GROUPS):
                    dve.wait_ge(stats_ready, GROUPS * n + g + 1)
                    nc.vector.bn_aggr(moments[:, g, :], stats[:, g, :]).then_inc(moments_ready, 1)

            def normalise(h, n):
                dve.wait_ge(rstd_ready, n + 1)
                if n:
                    dve.wait_ge(xT_mm, n)
                for g in range(GROUPS):
                    last = nc.vector.tensor_scalar(xnorm[:, g, :], resid[h][:, g, :], moments[:, g, 0:1],
                                                   rstd[:, g:g + 1], ALU.subtract, ALU.mult)
                last.then_inc(xnorm_ready, 1)

            def embed_rows(h):
                for g in range(GROUPS):
                    dve.wait_ge(tok_mm, GROUPS * h + (g + 1 if h == 0 else max(g + 1, 2)))
                    nc.vector.tensor_tensor(resid[h][:, g, :], tok_psum(h, g), table_sb[:, 0, :],
                                            ALU.add).then_inc(resid_ready, 1)
                    if g:
                        dve.wait_ge(resid_ready, GROUPS * h + g)
                        stats_of(h, g - 1)
                dve.wait_ge(resid_ready, GROUPS * (h + 1))
                stats_of(h, GROUPS - 1)

            def xT_lo_part(n):
                for k in range(KD):
                    dve.wait_ge(xT_hi, KD * n + k + 1)
                    at = slice(k * HPE, k * HPE + HP)
                    nc.vector.tensor_tensor(xT[n % 2][1][:, at], xT_bank(n, k)[:, 0:HP],
                                            as_f32(xT[n % 2][0][:, at]), ALU.subtract).then_inc(xT_lo, 1)

            def rotate(h, s):
                dve.wait_ge(qk_mm, 2 * h + s + 1)
                if h:
                    dve.wait_ge(qk_lo, 4 * (h - 1) + 2 * s + 2)
                for i, (parity, at) in enumerate(((0, C_COS), (1, C_SIN), (0, C_SIN), (1, C_COS))):
                    factor = cst[:, at:at + ROWS].unsqueeze(1).to_broadcast([P, HALF_IMAGES, ROWS])
                    nc.vector.tensor_tensor(rot[s][i][:].rearrange("p (b t) -> p b t", t=ROWS),
                                            rope_bank(s, parity)[:, 0:HT].rearrange("p (b t) -> p b t", t=ROWS),
                                            factor, ALU.mult).then_inc(rot_read, 1)

            def rotated_keys(h):
                dve.wait_ge(rot_read, 8 * (h + 1))
                nc.vector.tensor_tensor(rot[1][0][:], rot[1][0][:], rot[1][1][:], ALU.subtract).then_inc(rot_ready, 1)
                nc.vector.tensor_tensor(rot[1][2][:], rot[1][2][:], rot[1][3][:], ALU.add).then_inc(rot_ready, 1)

            def qk_lo_part(h, s):
                for parity in range(2):
                    dve.wait_ge(qk_hi, 4 * h + 2 * s + parity + 1)
                    at = (2 * parity + s) * HPE
                    nc.vector.tensor_tensor(qk[1][:, at:at + HT], rot[s][2 * parity][:],
                                            as_f32(qk[0][:, at:at + HT]), ALU.subtract).then_inc(qk_lo, 1)

            def v_lo_part(h):
                dve.wait_ge(v_hi, GROUPS * (h + 1))
                for g in range(GROUPS):
                    at = slice(g * D, (g + 1) * D)
                    nc.vector.tensor_tensor(val[1][0:GR, at], v_bank(h, g), as_f32(val[0][0:GR, at]),
                                            ALU.subtract).then_inc(v_lo, 1)

            def mask_scores(h):
                dve.wait_ge(s_mm, h + 1)
                if h:
                    dve.wait_ge(pT_mm, h)
                nc.vector.tensor_tensor(scores[:], score_bank(h)[0:GR, 0:GROUPS * GRE].rearrange("p (g t) -> p g t", t=GRE),
                                        cst[0:GR, C_MASK:C_MASK + GRE].unsqueeze(1).to_broadcast([GR, GROUPS, GRE]),
                                        ALU.add).then_inc(s_masked, 1)
                dve.wait_ge(s_masked, h + 1)
                nc.vector.tensor_reduce(top[:], scores[:], AX_X, ALU.max).then_inc(s_top, 1)
                dve.wait_ge(s_top, h + 1)
                dve.wait_ge(s_warm, 1)
                nc.vector.tensor_scalar(neg_top[:], top[:], -SCORE_SCALE, None, ALU.mult).then_inc(s_negtop, 1)

            def inv_sums(h):
                dve.wait_ge(p_ready, GROUPS * (h + 1))
                if h:
                    dve.wait_ge(h2_ready, GROUPS * h)
                nc.vector.reciprocal(inv_total[:], total[:]).then_inc(inv_ready, 1)

            def pT_lo_part(h):
                dve.wait_ge(pT_hi, h + 1)
                nc.vector.tensor_tensor(probsT[1][0:GR, :], pT_bank(h)[0:GR, 0:HP], as_f32(probsT[0][0:GR, :]),
                                        ALU.subtract).then_inc(pT_lo, 1)

            def add_attention(h):
                dve.wait_ge(pv_mm, h + 1)
                dve.wait_ge(inv_ready, h + 1)
                for g in range(GROUPS):
                    nc.vector.scalar_tensor_tensor(out=resid[h][:, g, :], in0=v_bank(h, g),
                                                   scalar=inv_total[:, g:g + 1], in1=resid[h][:, g, :],
                                                   op0=ALU.mult, op1=ALU.add).then_inc(h2_ready, 1)
                    if g:
                        dve.wait_ge(h2_ready, GROUPS * h + g)
                        stats_of(h, g - 1)
                dve.wait_ge(h2_ready, GROUPS * (h + 1))
                stats_of(h, GROUPS - 1)

            def choose(h):
                dve.wait_ge(gate_mm, h + 1)
                nc.vector.tensor_copy(logits[:].rearrange("p g e -> p (g e)"), logit_psum(h)).then_inc(logits_ready, 1)
                dve.wait_ge(logits_ready, h + 1)
                all_pairs = [GR, GROUPS, EXPERTS, EXPERTS]
                nc.vector.tensor_reduce(best[:, 0, :], logits[:], AX_X, ALU.max).then_inc(s_chain, 1)
                chain[0] += 1
                link(nc.vector.tensor_tensor(versus[:], logits[:].unsqueeze(2).to_broadcast(all_pairs),
                                             logits[:].unsqueeze(3).to_broadcast(all_pairs), ALU.subtract))
                order = cst[0:GR, C_ORDER:C_ORDER + EXPERTS * EXPERTS]
                link(nc.vector.tensor_tensor(versus[:].rearrange("p g e j -> p g (e j)"),
                                             versus[:].rearrange("p g e j -> p g (e j)"),
                                             order.unsqueeze(1).to_broadcast([GR, GROUPS, EXPERTS * EXPERTS]), ALU.is_ge))
                link(nc.vector.tensor_reduce(place[:], versus[:], AX_X, ALU.add))
                link(nc.vector.scalar_tensor_tensor(out=second[:], in0=place[:], scalar=1.0, in1=logits[:],
                                                    op0=ALU.is_equal, op1=ALU.mult))
                link(nc.vector.tensor_reduce(best[:, 1, :], second[:], AX_X, ALU.add))
                if h:
                    dve.wait_ge(tanh_ready, h)
                nc.vector.tensor_tensor(gap[:], best[:, 0, :], best[:, 1, :], ALU.subtract).then_inc(gap_ready, 1)
                if h:
                    dve.wait_ge(mask_mm, h)
                for s in range(2):
                    nc.vector.tensor_scalar(chosen_x[:, s], place[:].unsqueeze(3).to_broadcast([GR, GROUPS, EXPERTS, RANK]),
                                            float(s), LORA_SCALE, ALU.is_equal, ALU.mult).then_inc(chosen_ready, 1)

            def weigh(h):
                dve.wait_ge(tanh_ready, h + 1)
                for s, sign in enumerate((0.5, -0.5)):
                    nc.vector.tensor_scalar(slot_w[:, s, :], gap_tanh[:], sign, 0.5, ALU.mult, ALU.add).then_inc(s_chain, 1)
                chain[0] += 2
                dve.wait_ge(s_chain, chain[0])
                if h:
                    dve.wait_ge(weight_mm, h)
                nc.vector.tensor_copy(slot_wx[:], slot_w[:].unsqueeze(3).to_broadcast([GR, 2, GROUPS, P])).then_inc(slots_ready, 1)

            def slot_inputs(h):
                dve.wait_ge(ranks_ready, 2 * (h + 1))
                for s in range(2):
                    dve.wait_ge(mask_ready, 2 * h + s + 1)
                    nc.vector.tensor_tensor(slot_in[:, s, :, :], ranks[:],
                                            mask[h][:, s, :].unsqueeze(1).to_broadcast([P, 2, HT]),
                                            ALU.mult).then_inc((slot_in_ready, slot_masked)[s], 1)
                dve.wait_ge(slot_in_ready, 2 * h + 1)
                dve.wait_ge(slot_masked, h + 1)
                nc.vector.tensor_tensor(slot_in[:, 1, :, :], slot_in[:, 1, :, :], slot_in[:, 0, :, :],
                                        ALU.subtract).then_inc(slot_in_ready, 1)

            def slot_lo_part(h):
                for s in range(2):
                    dve.wait_ge(slot_hi, 2 * h + s + 1)
                    at = slice(2 * s * HT, 2 * (s + 1) * HT)
                    nc.vector.tensor_tensor(slot_inr[1][:, at], slot_in[:, s].rearrange("p w t -> p (w t)"),
                                            as_f32(slot_inr[0][:, at]), ALU.subtract).then_inc(slot_lo, 1)

            def gated(n, slot):
                if slot == 0:
                    dve.wait_ge(silu1, n + 1)
                    dve.wait_ge(up1_mm, n + 1)
                else:
                    dve.wait_ge(silu2, n + 1)
                    dve.wait_ge(up2_mm, n + 1)
                at = act_ring[:, n % 2, slot, :]
                nc.vector.tensor_tensor(at, up_bank(n, 1)[:, 0:HT], at, ALU.mult).then_inc((act1, act2)[slot], 1)

            def lo_parts(n):
                if n >= 2:
                    dve.wait_ge(down_mm, n - 1)
                dve.wait_ge(act_hi, n + 1)
                nc.vector.tensor_tensor(actr[n % 2][1][:], act_ring[:, n % 2, :, :].rearrange("p s t -> p (s t)"),
                                        as_f32(actr[n % 2][0][:]), ALU.subtract).then_inc(act_lo, 1)
                dve.wait_ge(mix_hi, n + 1)
                nc.vector.tensor_tensor(mixr[n % 2][1][:], mix_ring[:, n % 2, :], as_f32(mixr[n % 2][0][:]),
                                        ALU.subtract).then_inc(mix_lo, 1)

            def low_sums(h):
                dve.wait_ge(down_mm, FT * (h + 1))
                dve.wait_ge(slot_lo, 2 * HALVES)
                if h:
                    dve.wait_ge(s_out, 16 * h)
                for s in range(2):
                    nc.vector.tensor_tensor(low[:, s, :], low_bank[s][:, 0:HT], mask[h][:, s, :],
                                            ALU.mult).then_inc(low_masked, 1)
                dve.wait_ge(low_masked, 2 * (h + 1))
                if h:
                    dve.wait_ge(low_lo, h)
                nc.vector.tensor_tensor(low_sum, low[:, 0, :], low[:, 1, :], ALU.add).then_inc(low_ready, 1)

            def low_lo_part(h):
                dve.wait_ge(low_hi, h + 1)
                nc.vector.tensor_tensor(lowr[1][:], low_sum, as_f32(lowr[0][:]), ALU.subtract).then_inc(low_lo, 1)

            def y_copy(h):
                dve.wait_ge(y_mm, h + 1)
                nc.vector.tensor_copy(yT[:, 1, :], y_bank(h, 1)[:, 0:HT]).then_inc(y_dve, 1)

            for i in range(3):
                lo_part(f"x0_{i}")
            dve.wait_ge(s_table, 16)
            nc.vector.tensor_tensor(table_sb[:, 0, :], table_sb[:, 0, :], table_sb[:, 1, :], ALU.add).then_inc(s_rows, 1)
            dve.wait_ge(s_rows, 1)
            embed_rows(0)
            moments_of(0)
            lo_part("x1_0")
            normalise(0, 0)
            dve.wait_ge(vo_hi, 1)
            nc.vector.tensor_tensor(vo[1][:], vo_bank[:, :], as_f32(vo[0][:]), ALU.subtract).then_inc(vo_lo, 1)
            lo_part("x1_1")
            dve.wait_ge(s_const, 16)
            nc.vector.tensor_copy(ident_bf[:], ident).then_inc(s_ident, 1)
            xT_lo_part(0)
            lo_part("x1_2")
            rotate(0, 0)
            rotate(0, 1)
            rotated_keys(0)
            qk_lo_part(0, 0)
            qk_lo_part(0, 1)
            v_lo_part(0)
            mask_scores(0)
            embed_rows(1)
            moments_of(1)
            inv_sums(0)
            pT_lo_part(0)
            normalise(1, 1)
            add_attention(0)
            moments_of(2)
            xT_lo_part(1)
            normalise(0, 2)
            rotate(1, 0)
            xT_lo_part(2)
            rotate(1, 1)
            choose(0)
            rotated_keys(1)
            weigh(0)
            slot_inputs(0)
            slot_lo_part(0)
            qk_lo_part(1, 0)
            qk_lo_part(1, 1)
            v_lo_part(1)
            mask_scores(1)
            for n in range(NS + 1):
                if n == FT:
                    slot_lo_part(1)
                if n < NS:
                    gated(n, 0)
                if n >= 1:
                    lo_parts(n - 1)
                if n < NS:
                    gated(n, 1)
                if n == 0:
                    inv_sums(1)
                    pT_lo_part(1)
                elif n == 1:
                    add_attention(1)
                    moments_of(3)
                elif n == 2:
                    normalise(1, 3)
                elif n == 3:
                    xT_lo_part(3)
                elif n == 4:
                    choose(1)
                elif n == 5:
                    weigh(1)
                elif n == 6:
                    slot_inputs(1)
                elif n == FT + 1:
                    low_sums(0)
                    low_lo_part(0)
                elif n == FT + 2:
                    y_copy(0)
            low_sums(1)
            low_lo_part(1)
            y_copy(1)

        @block.tensor
        def _(pe):
            def product(dst, w, x, start, stop, open_bank=False):
                nc.tensor.matmul(dst, w[0], x[0], start=start, stop=False, skip_group_check=open_bank)
                nc.tensor.matmul(dst, w[0], x[1], start=False, stop=False, skip_group_check=open_bank)
                return nc.tensor.matmul(dst, w[1], x[0], start=False, stop=stop, skip_group_check=open_bank)

            def cols(parts, a, b, rows=P):
                return [p[0:rows, a:b] for p in parts]

            def split(name):
                pe.wait_ge(hi_done, NAMES.index(name) + 1)
                pe.wait_ge(lo_done[name], 1)

            def embedding(h, tiles):
                for k in tiles:
                    if k % (KX // 3) == 0:
                        split(f"x{h}_{k // (KX // 3)}")
                        split(f"w{k // (KX // 3)}")
                order = [(k, g) for k in tiles for g in range(GROUPS)]
                if h == 0 and KX - 1 in tiles:
                    order = [(k, g) for g in range(GROUPS) for k in tiles]
                for k, g in order:
                    at = k * HP + g * GR
                    last = product(tok_psum(h, g), cols(xhalf[h], at, at + GR),
                                   cols(embed, k * D, (k + 1) * D), k == 0 and (h, g) != (1, 1), k == KX - 1, h == 1)
                    if k == KX - 1:
                        last.then_inc(tok_mm, 1)

            def value_out():
                split("valout")
                for m in range(KD):
                    for k in range(KD):
                        last = product(vo_bank[:, m * D:(m + 1) * D], cols(valout, k * D + m * P, k * D + (m + 1) * P),
                                       cols(valout, (KD + k) * D, (KD + k + 1) * D), k == 0, k == KD - 1)
                last.then_inc(vo_mm, 1)

            def transpose_rows(n):
                pe.wait_ge(xnorm_ready, n + 1)
                pe.wait_ge(s_const, 16)
                for k in range(KD):
                    for g in range(GROUPS):
                        last = nc.tensor.transpose(xT_bank(n, k)[:, g * GR:(g + 1) * GR],
                                                   xnorm[:, g, k * P:(k + 1) * P], ident[0:GR, 0:GR])
                last.then_inc(xT_mm, 1)

            def queries_keys(h, s):
                split("qk_w")
                pe.wait_ge(xT_lo, KD * (h + 1))
                if h == 0:
                    pe.wait_ge(vo_lo, 1)
                    pe.wait_ge(resid_ready, GROUPS)
                elif s == 0:
                    pe.wait_ge(rot_read, 4)
                else:
                    pe.wait_ge(s_masked, 1)
                    pe.wait_ge(pT_lo, 1)
                for parity in range(2):
                    for k in range(KD):
                        at = M_QK + (k * 4 + 2 * parity + s) * P
                        last = product(rope_bank(s, parity)[:, 0:HT], cols(small, at, at + P),
                                       cols(xT[h], k * HPE, k * HPE + HT), k == 0, k == KD - 1)
                last.then_inc(qk_mm, 1)

            def values(h):
                pe.wait_ge(vo_lo, 1)
                if h == 0:
                    pe.wait_ge(xT_lo, KD)
                else:
                    pe.wait_ge(rot_read, 8 * h + 4)
                for g in range(GROUPS):
                    for k in range(KD):
                        at = k * HPE + g * GR
                        last = product(v_bank(h, g), cols(xT[h], at, at + GR), cols(vo, k * D, (k + 1) * D),
                                       k == 0, k == KD - 1)
                last.then_inc(v_mm, 1)

            def score(h):
                pe.wait_ge(qk_lo, 4 * (h + 1))
                pe.wait_ge(s_pads, 1)
                if h == 0:
                    pe.wait_ge(rot_read, 8)
                else:
                    pe.wait_ge(v_lo, GROUPS * (h + 1))
                for g in range(GROUPS):
                    for k in range(KD):
                        q, key = 2 * k * HPE + g * GR, (2 * k + 1) * HPE + g * GR
                        last = product(score_bank(h)[0:GR, g * GRE:(g + 1) * GRE], cols(qk, q, q + GR),
                                       cols(qk, key, key + GRE), k == 0, k == KD - 1)
                last.then_inc(s_mm, 1)

            def transpose_probs(h):
                pe.wait_ge(p_ready, GROUPS * (h + 1))
                for g in range(GROUPS):
                    last = nc.tensor.transpose(pT_bank(h)[0:GR, g * GR:(g + 1) * GR], scores[:, g, 0:GR],
                                               ident[0:GR, 0:GR])
                last.then_inc(pT_mm, 1)

            def weighted_values(h):
                pe.wait_ge(pT_lo, h + 1)
                pe.wait_ge(v_lo, GROUPS * (h + 1))
                if h:
                    pe.wait_ge(s_masked, h + 1)
                for g in range(GROUPS):
                    last = product(v_bank(h, g), cols(probsT, g * GR, (g + 1) * GR, GR),
                                   cols(val, g * D, (g + 1) * D, GR), True, True)
                last.then_inc(pv_mm, 1)

            def router(h):
                split("rest_w")
                pe.wait_ge(xT_lo, KD * (h + 3))
                if h == 0:
                    pe.wait_ge(xT_lo, 2 * KD)
                x = xT[h]
                for g in range(GROUPS):
                    for k in range(KD):
                        at, gt = k * HPE + g * GR, M_GATE + k * EXPERTS
                        last = product(logit_psum(h)[:, g * EXPERTS:(g + 1) * EXPERTS], cols(x, at, at + GR),
                                       cols(small, gt, gt + EXPERTS), k == 0, k == KD - 1)
                last.then_inc(gate_mm, 1)

            def rank_products(h):
                x = xT[h]
                for w in range(2):
                    if w == 1:
                        pe.wait_ge(logits_ready, h + 1)
                    for k in range(KD):
                        at = M_A13 + (k * 2 + w) * P
                        last = product(rank_bank(h, w)[:, 0:HT], cols(small, at, at + P),
                                       cols(x, k * HPE, k * HPE + HT), k == 0, k == KD - 1)
                last.then_inc(ranks_mm, 1)

            def spread_masks(h):
                pe.wait_ge(chosen_ready, 2 * (h + 1))
                pe.wait_ge(s_ident, 1)
                if h == 0:
                    pe.wait_ge(rot_read, 16)
                else:
                    pe.wait_ge(ranks_ready, 2 * (h + 1))
                for s in range(2):
                    for g in range(GROUPS):
                        rows = group_rows(g)
                        last = nc.tensor.matmul(mask_bank(h, s)[:, g * GR:g * GR + rows],
                                                chosen_x[:, s, g].rearrange("p e r -> p (e r)"), ident_bf[0:GR, 0:rows],
                                                start=True, stop=True)
                last.then_inc(mask_mm, 1)

            def spread_weights(h):
                pe.wait_ge(slots_ready, h + 1)
                if h == 0:
                    pe.wait_ge(ranks_ready, 2)
                else:
                    pe.wait_ge(mask_ready, 2 * (h + 1))
                for s in range(2):
                    for g in range(GROUPS):
                        rows = group_rows(g)
                        last = nc.tensor.matmul(weight_bank(h, s)[:, g * GR:g * GR + rows], slot_wx[:, s, g, :],
                                                ident[0:GR, 0:rows], start=True, stop=True)
                last.then_inc(weight_mm, 1)

            def ffn_cols(t, at):
                return cols(ffn[t], at, at + P)

            def common(n, w):
                h, t = divmod(n, FT)
                if n == 0:
                    pe.wait_ge(xT_lo, 3 * KD)
                elif n == UP_PAIRS_FROM:
                    pe.wait_ge(y_act, 1)
                    pe.wait_ge(y_dve, 1)
                else:
                    pe.wait_ge((silu2, act2)[w], n if n < UP_PAIRS_FROM else n - 1)
                if h == 0 and w == 0:
                    split(f"ffn{t}")
                for k in range(KD):
                    product(up_bank(n, w)[:, 0:HT], ffn_cols(t, T_UP + (w * KD + k) * P),
                            cols(xT[h], k * HPE, k * HPE + HT), k == 0, False)

            def slot_part(n, slot, w):
                h, t = divmod(n, FT)
                if t == 0 and w == 0:
                    pe.wait_ge(slot_lo, 2 * h + slot + 1)
                if slot == 1:
                    pe.wait_ge((silu1, act1)[w], n + 1)
                x = (2 * slot + w) * HT
                product(up_bank(n, w)[:, 0:HT], ffn_cols(t, T_B13 + w * P), cols(slot_inr, x, x + HT),
                        False, True, slot == 1).then_inc(((gate1_mm, up1_mm), (gate2_mm, up2_mm))[slot][w], 1)

            def residual(h):
                pe.wait_ge(weight_ready, 2 * (h + 1))
                for m in range(KD):
                    for g in range(GROUPS):
                        rows = group_rows(g)
                        nc.tensor.matmul(y_bank(h, m)[:, g * GR:g * GR + rows], resid[h][:, g, m * P:(m + 1) * P],
                                         ident[0:GR, 0:rows], start=(g == 0), stop=False, skip_group_check=True)

            def down_ranks(n):
                h, t = divmod(n, FT)
                if t == 0:
                    if h == 0:
                        pe.wait_ge(mask_ready, 2)
                    else:
                        pe.wait_ge(low_masked, 2 * h)
                pe.wait_ge(act_lo, n + 1)
                for s in range(2):
                    product(low_bank[s][:, 0:HT], ffn_cols(t, T_A2), cols(actr[n % 2], s * HT, (s + 1) * HT),
                            t == 0, t == FT - 1)

            def down(n):
                h, t = divmod(n, FT)
                if t == 0:
                    residual(h)
                pe.wait_ge(mix_lo, n + 1)
                for m in range(KD):
                    last = product(y_bank(h, m)[:, 0:HT], ffn_cols(t, T_DOWN + m * P),
                                   cols(mixr[n % 2], 0, HT), False, False, True)
                last.then_inc(down_mm, 1)

            def low_out(h):
                pe.wait_ge(low_lo, h + 1)
                for m in range(KD):
                    at = M_B2 + m * P
                    last = product(y_bank(h, m)[:, 0:HT], cols(small, at, at + P), cols(lowr, 0, HT), False, True, True)
                last.then_inc(y_mm, 1)

            embedding(0, range(0, 4))
            embedding(0, range(4, KX))
            value_out()
            embedding(1, range(0, 2))
            transpose_rows(0)
            embedding(1, range(2, 3))
            queries_keys(0, 0)
            queries_keys(0, 1)
            values(0)
            embedding(1, range(3, 5))
            score(0)
            embedding(1, range(5, 6))
            transpose_probs(0)
            weighted_values(0)
            transpose_rows(1)
            queries_keys(1, 0)
            queries_keys(1, 1)
            transpose_rows(2)
            router(0)
            rank_products(0)
            common(0, 0)
            spread_masks(0)
            common(0, 1)
            spread_weights(0)
            values(1)
            slot_part(0, 0, 0)
            slot_part(0, 0, 1)
            score(1)
            for n in range(NS + 2):
                if n < NS and n % FT == 0 and n > 0:
                    common(n, 0)
                    common(n, 1)
                    slot_part(n, 0, 0)
                    slot_part(n, 0, 1)
                elif 0 < n < NS:
                    common(n, 0)
                    slot_part(n, 0, 0)
                    common(n, 1)
                    slot_part(n, 0, 1)
                if n < NS:
                    slot_part(n, 1, 0)
                if n >= 2:
                    down_ranks(n - 2)
                if n < NS:
                    slot_part(n, 1, 1)
                if n >= 2:
                    down(n - 2)
                if n == 0:
                    transpose_probs(1)
                    weighted_values(1)
                elif n == 2:
                    transpose_rows(3)
                elif n == 4:
                    router(1)
                elif n == 5:
                    rank_products(1)
                    spread_masks(1)
                elif n == 6:
                    spread_weights(1)
                elif n == FT + 2:
                    low_out(0)
            low_out(1)


def kernel(x, L0_tok_W, L0_tok_b, L0_tok_cls_token, L0_tok_pos_enc, L0_attn_wq, L0_attn_wk, L0_attn_wv, L0_attn_wo,
           L0_ffn_gate_w, L0_ffn_w_gate, L0_ffn_w_up, L0_ffn_w_down, L0_ffn_A1, L0_ffn_B1, L0_ffn_A3, L0_ffn_B3,
           L0_ffn_A2, L0_ffn_B2):
    import concourse.bacc as bacc
    from concourse.bass_utils import run_bass_kernel_spmd

    x = np.asarray(x)
    f32 = np.float32

    def tiles(a):
        return a.reshape(-1, P, a.shape[1]).transpose(1, 0, 2)

    def flat(a):
        return a.reshape(P, -1)

    rows = x.reshape(IMAGES, CHANNELS, GRID, PATCH, GRID, PATCH).transpose(0, 2, 4, 1, 3, 5)
    rows = rows.reshape(HALVES, HALF_IMAGES, ROWS - 1, KX * P)
    padded = np.zeros((HALVES, GROUPS * GROUP_IMAGES, ROWS, KX * P), f32)
    padded[:, :HALF_IMAGES, 1:] = rows
    patches = padded.reshape(HALVES, HP, KX, P).transpose(3, 0, 2, 1).reshape(P, HALVES, KX * HP)

    embed_w = flat(tiles(np.asarray(L0_tok_W).T))
    wv, wo = np.asarray(L0_attn_wv), np.asarray(L0_attn_wo)
    value_w = np.concatenate([flat(tiles(wv)), flat(tiles(wo.T))], axis=1)
    qT, kT = np.asarray(L0_attn_wq).T, np.asarray(L0_attn_wk).T
    qk = np.stack([qT[:, 0::2], kT[:, 0::2], qT[:, 1::2], kT[:, 1::2]], axis=1).reshape(D, 4 * P)
    ranks_first = lambda a: np.asarray(a).reshape(EXPERTS * RANK, -1).T
    a13 = np.concatenate([ranks_first(L0_ffn_A1), ranks_first(L0_ffn_A3)], axis=1)
    by_rank = lambda b: np.asarray(b).transpose(0, 2, 1).reshape(EXPERTS * RANK, -1)
    small_w = np.concatenate([flat(tiles(qk)), flat(tiles(a13)), flat(tiles(np.asarray(L0_ffn_gate_w).T)),
                              by_rank(L0_ffn_B2)], axis=1)
    up = np.stack([np.asarray(L0_ffn_w_gate).T, np.asarray(L0_ffn_w_up).T])
    up = up.reshape(2, KD, P, FT, P).transpose(2, 3, 0, 1, 4).reshape(P, FT, -1)
    b13 = np.stack([by_rank(L0_ffn_B1), by_rank(L0_ffn_B3)]).reshape(2, P, FT, P).transpose(1, 2, 0, 3).reshape(P, FT, -1)
    a2 = tiles(ranks_first(L0_ffn_A2))
    dn = tiles(np.asarray(L0_ffn_w_down).T)
    ffn_w = np.concatenate([up, b13, a2, dn], axis=2)

    pos = np.tile(np.asarray(L0_tok_pos_enc)[0], (GROUP_IMAGES, 1))
    image = np.tile(np.asarray(L0_tok_b)[None, :], (ROWS, 1))
    image[0] = np.asarray(L0_tok_cls_token)[0, 0]
    table = np.stack([pos, np.tile(image, (GROUP_IMAGES, 1))], axis=1)

    const = np.zeros((P, C_ALL), f32)
    const[:, C_ID:C_ID + P] = np.eye(P, dtype=f32)
    i, j = np.arange(P)[:, None] // ROWS, np.arange(GRE)[None, :] // ROWS
    const[:, C_MASK:C_MASK + GRE] = np.where(i == j, 0.0, FAR)
    inv = (f32(1.0) / f32(10000.0) ** (np.arange(0, D, 2, dtype=f32) / f32(D))).astype(f32)
    angle = np.outer(inv, np.arange(ROWS, dtype=f32)).astype(f32)
    const[:, C_COS:C_COS + ROWS] = np.cos(angle)
    const[:, C_SIN:C_SIN + ROWS] = np.sin(angle)
    e, other = np.arange(EXPERTS)[:, None], np.arange(EXPERTS)[None, :]
    const[:, C_ORDER:] = np.where(other < e, 0.0, LEAST).astype(f32).reshape(1, -1)

    arrays = {"patches": patches, "embed_w": embed_w, "value_w": value_w, "small_w": small_w, "ffn_w": ffn_w,
              "const": const, "table": table}
    arrays = {k: np.ascontiguousarray(v) for k, v in arrays.items()}
    nc = bacc.Bacc("TRN2", target_bir_lowering=False, num_devices=1, dynamic_dma_scratch_size=1024)
    args = [nc.dram_tensor(k, v.shape, F32, kind="ExternalInput").ap() for k, v in arrays.items()]
    out = nc.dram_tensor("out", (P, HALVES, KD, HT), F32, kind="ExternalOutput").ap()
    vit_block(nc, *args, out)
    r = run_bass_kernel_spmd(nc, [arrays], core_ids=[0])
    got = r.results[0]["out"]
    return np.ascontiguousarray(got.transpose(1, 3, 2, 0).reshape(IMAGES, ROWS, D))
```

```python
from contextlib import ExitStack

import numpy as np
import concourse.bass as bass
from concourse import mybir

ALU = mybir.AluOpType
ACT = mybir.ActivationFunctionType
AX_X = mybir.AxisListType.X
F32 = mybir.dt.float32
F32R = mybir.dt.float32r
BF16 = mybir.dt.bfloat16

P = 128
IMAGES, CHANNELS, SIDE, PATCH = 16, 3, 96, 16
D = 256
F = 1024
EXPERTS, RANK = 8, 16
GRID = SIDE // PATCH
ROWS = GRID * GRID + 1
HALVES = 2
HALF_IMAGES = IMAGES // HALVES
GROUP_IMAGES = 3
GROUPS = -(-HALF_IMAGES // GROUP_IMAGES)
GR = GROUP_IMAGES * ROWS
GRE = GR + 1
HT = HALF_IMAGES * ROWS
HP = GROUPS * GR
HPE = HP + 1
KX = CHANNELS * PATCH * PATCH // P
KD = D // P
FT = F // P
EPS = 1e-5
SCORE_SCALE = float(D) ** -0.5
LORA_SCALE = 2.0
FAR = -1e30
LEAST = 1.1754944e-38

C_ID, C_MASK = 0, P
C_COS = C_MASK + GRE
C_SIN = C_COS + ROWS
C_ORDER = C_SIN + ROWS
C_ALL = C_ORDER + EXPERTS * EXPERTS
M_QK = 0
M_A13 = M_QK + KD * 4 * P
M_GATE = M_A13 + KD * 2 * P
M_B2 = M_GATE + KD * EXPERTS
M_ALL = M_B2 + KD * P
T_UP = 0
T_B13 = T_UP + 2 * KD * P
T_A2 = T_B13 + 2 * P
T_DOWN = T_A2 + P
T_ALL = T_DOWN + KD * P
NS = HALVES * FT
UP_PAIRS_FROM = FT + 5
WARM_UP = 8
PIECES = ((0, 1, 2, 4, KX), (0, 2, 4, KX))
EARLY_IN = (1, 2, 3)
STAGES = 5
STAGE = T_ALL


def vit_block(nc, patches, embed_w, value_w, small_w, ffn_w, const, table, out):
    ctx = ExitStack()
    with ctx:
        def sb(name, shape, dt=F32, where=ctx):
            return where.enter_context(nc.sbuf_tensor(name, shape, dt))

        def pair(name, cols, where=ctx):
            return [sb(f"{name}_{part}", [P, cols], F32R, where) for part in ("hi", "lo")]

        def sem(name):
            return ctx.enter_context(nc.semaphore(name))

        def as_f32(ap):
            return ap.bitcast(F32)

        cst = sb("cst", [P, C_ALL])
        table_sb = sb("table_sb", [GR, 2, D])
        ident_bf = sb("ident_bf", [P, P], BF16)
        stage = [sb(f"stage{i}", [P, STAGE]) for i in range(STAGES)]
        small = pair("small", M_ALL)
        vo = pair("vo", KD * D)
        resid = [sb(f"resid{h}", [GR, GROUPS, D]) for h in range(HALVES)]
        xnorm = [sb(f"xnorm{i}", [GR, GROUPS, D]) for i in range(2)]
        xT = [pair(f"xT{h}", KD * HPE) for h in range(HALVES)]
        stats = sb("stats", [GR, 2, GROUPS, 6])
        moments = sb("moments", [GR, 2, GROUPS, 2])
        spread = sb("spread", [GR, 2, GROUPS])
        minus_half = sb("minus_half", [GR, GROUPS])
        rstd = sb("rstd", [GR, 2, GROUPS])
        shift = sb("shift", [GR, GROUPS])
        rot = [[sb(f"rot{s}_{i}", [P, HT]) for i in range(4)] for s in range(2)]
        val = pair("val", GROUPS * D)
        neg_top = sb("neg_top", [GR, GROUPS])
        total = sb("total", [GR, GROUPS])
        inv_total = sb("inv_total", [GR, GROUPS])
        logits = sb("logits", [GR, GROUPS, EXPERTS])
        versus = sb("versus", [GR, GROUPS, EXPERTS, EXPERTS])
        place = sb("place", [GR, GROUPS, EXPERTS])
        second = sb("second", [GR, GROUPS, EXPERTS])
        best = sb("best", [GR, 2, GROUPS])
        gap = sb("gap", [GR, GROUPS])
        gap_tanh = sb("gap_tanh", [GR, GROUPS])
        slot_w = sb("slot_w", [GR, 2, GROUPS])
        slot_wx = sb("slot_wx", [GR, 2, GROUPS, P])
        chosen_x = sb("chosen_x", [GR, 2, GROUPS, EXPERTS, RANK], BF16)
        ranks = sb("ranks", [P, 2, HT])
        mask = [sb(f"mask{h}", [P, 2, HT]) for h in range(HALVES)]
        weight = sb("weight", [P, 2, HT])
        slot_in = sb("slot_in", [P, 2, 2, HT])
        slot_inr = pair("slot_inr", 4 * HT)
        zeros = slot_inr[0][:, 0:512]
        act_ring = sb("act_ring", [P, 2, 2, HT])
        actr = [pair(f"actr{i}", 2 * HT) for i in range(2)]
        mix_ring = sb("mix_ring", [P, 2, HT])
        mixr = [pair(f"mixr{i}", HT) for i in range(2)]
        lowr = pair("lowr", HT)
        low, low_sum, yT = slot_in[:, 0], slot_in[:, 1, 0], slot_in[:, 0]
        with ExitStack() as early:
            xhalf = [pair("xhalf0", KX * HP, early)]
        with ExitStack() as attn:
            qk = pair("qk", 4 * HPE, attn)
            scores = sb("scores", [GR, GROUPS, GRE], F32, attn)
            probsT = pair("probsT", HP, attn)
        over = max(2 * KX * HP, 2 * 4 * HPE + GROUPS * GRE + 2 * HP)
        sb("overlaid", [P, over])
        ffn = [pair(f"ffn{t}", T_ALL) for t in range(EARLY_IN[0])]
        with ExitStack() as early:
            early_at = [sb(f"early{i}", [P, T_ALL], F32, early) for i in range(2 * len(EARLY_IN))]
        ffn += [pair(f"ffn{t}", T_ALL) for t in EARLY_IN]
        with ExitStack() as early:
            xhalf.append(pair("xhalf1", KX * HP, early))
            embed = pair("embed", KX * D, early)
            valout = pair("valout", 2 * KD * D, early)
        ffn += [pair(f"ffn{t}", T_ALL) for t in range(FT // 2, FT)]

        bank = [ctx.enter_context(nc.psum_tensor(f"bank{i}", [P, 512], F32)) for i in range(8)]

        def part_of(parts, a, b):
            return [p[:, a:b] for p in parts]

        def embed_load(i):
            at = [k * D for k in PIECES[0][i:i + 2]]
            return (f"w{i}", embed_w[:, at[0]:at[1]], part_of(embed, *at))

        def patch_load(h, i):
            at = [k * HP for k in PIECES[h][i:i + 2]]
            return (f"x{h}_{i}", patches[:, h, at[0]:at[1]], part_of(xhalf[h], *at))

        LOADS = [load for i in range(len(PIECES[0]) - 1) for load in (embed_load(i), patch_load(0, i))]
        LOADS += [patch_load(1, 0), patch_load(1, 1)]
        half_qk = M_A13 // 2
        LOADS += [("q_w", small_w[:, 0:half_qk], part_of(small, 0, half_qk)),
                  ("k_w", small_w[:, half_qk:M_A13], part_of(small, half_qk, M_A13)),
                  ("valout", value_w, part_of(valout, 0, 2 * KD * D)), patch_load(1, 2)]
        LOADS += [("rest_w", small_w[:, M_A13:M_ALL], part_of(small, M_A13, M_ALL))]
        LOADS += [(f"ffn{t}", ffn_w[:, t, :], part_of(ffn[t], 0, T_ALL)) for t in range(FT)]
        NAMES = [name for name, *_ in LOADS]
        EARLY = len(early_at)

        def place_of(i):
            return (i, 1) if i < EARLY else (EARLY + (i - EARLY) % STAGES, (i - EARLY) // STAGES + 1)

        places = early_at + stage
        load_at = {name: (places[place_of(i)[0]][:, 0:src.shape[1]], src, parts)
                   for i, (name, src, parts) in enumerate(LOADS)}
        loaded = [sem(f"place{i}_loaded") for i in range(len(places))]
        hi_done = sem("staged_hi_done")
        lo_done = {name: sem(f"{name}_lo_done") for name in NAMES}

        s_const, s_table = sem("const_loaded"), sem("table_loaded")
        s_rows, s_ident, s_pads, s_mhalf = sem("table_summed"), sem("ident_bf_ready"), sem("pads_cleared"), sem("minus_half_ready")
        tok_mm, tok_copied, resid_ready = sem("tok_mm"), sem("tok_copied"), sem("resid_ready")
        vo_mm, vo_hi, vo_lo = sem("vo_mm"), sem("vo_hi_ready"), sem("vo_lo_ready")
        stats_ready, moments_ready, spread_ready = sem("stats_ready"), sem("moments_ready"), sem("spread_ready")
        rstd_ready, xnorm_ready, shift_ready = sem("rstd_ready"), sem("xnorm_ready"), sem("shift_ready")
        xT_mm, xT_hi, xT_lo = sem("xT_mm"), sem("xT_hi_ready"), sem("xT_lo_ready")
        qk_mm, rot_read, rot_ready = sem("qk_mm"), sem("rot_read"), [sem("queries_rotated"), sem("keys_rotated")]
        qk_hi, queries_lo, keys_lo = sem("qk_hi_ready"), sem("queries_lo_ready"), sem("keys_lo_ready")
        v_mm, v_hi, v_lo = sem("v_mm"), sem("v_hi_ready"), sem("v_lo_ready")
        s_mm, s_masked, s_negtop = sem("scores_mm"), sem("scores_masked"), sem("neg_top_ready")
        p_ready, inv_ready = sem("probs_ready"), sem("inv_total_ready")
        pT_mm, pT_hi, pT_lo, pv_mm = sem("pT_mm"), sem("pT_hi_ready"), sem("pT_lo_ready"), sem("pv_mm")
        h2_ready = sem("h2_ready")
        gate_mm, ranks_mm, logits_ready = sem("gate_mm"), sem("ranks_mm"), sem("logits_ready")
        gap_ready, tanh_ready, slots_ready = sem("gap_ready"), sem("gap_tanh_ready"), sem("slots_ready")
        chosen_ready = sem("chosen_ready")
        ranks_ready = sem("ranks_ready")
        mask_mm, mask_ready = sem("mask_mm"), sem("mask_ready")
        weight_mm, weight_ready = sem("weight_mm"), sem("weight_ready")
        slot_in_ready, slot_hi, slot_lo = sem("slot_in_ready"), sem("slot_hi_ready"), sem("slot_lo_ready")
        mask2_ready = sem("mask2_ready")
        gate1_mm, up1_mm, gate2_mm, up2_mm = sem("gate1_mm"), sem("up1_mm"), sem("gate2_mm"), sem("up2_mm")
        silu1, silu2, act1, act2 = sem("silu1_done"), sem("silu2_done"), sem("act1_done"), sem("act2_done")
        last_actw = sem("last_act_weighted")
        actw, act_hi, act_lo = sem("act_weighted"), sem("act_hi_ready"), sem("act_lo_ready")
        mixed, mix_hi, mix_lo = sem("mixed"), sem("mix_hi_ready"), sem("mix_lo_ready")
        down_mm, low_mm = sem("down_mm"), sem("low_mm")
        low_masked, low_ready, low_hi, low_lo = sem("low_masked"), sem("low_ready"), sem("low_hi_ready"), sem("low_lo_ready")
        y_mm, y_act, y_dve, s_out = sem("y_mm"), sem("y_act_copied"), sem("y_dve_copied"), sem("stored")
        s_chain = sem("dve_chain")
        s_warm, s_zeros = sem("table_warm"), sem("zeros_ready")

        ident = cst[:, C_ID:C_ID + P]

        def tok_psum(h, g):
            return bank[g][0:GR, 0:D] if h == 0 else bank[4 + g // 2][0:GR, (g % 2) * D:(g % 2) * D + D]

        vo_bank = bank[1]

        def up_bank(n, w):
            return bank[4 * (n % 2) * (n == 1 or n >= UP_PAIRS_FROM) + w]

        low_bank = bank[2:4]

        def y_bank(h, m):
            return bank[(4, 6)[h] + m]

        def xT_bank(n, k):
            return bank[(0, 4, 0, 6)[n] + k]

        def rope_bank(s, parity):
            return bank[(6, 2)[s] + parity]

        def v_bank(h, g):
            return bank[(0, 6)[h] + g // 2][0:GR, (g % 2) * D:(g % 2) * D + D]

        def score_bank():
            return bank[2]

        def pT_bank():
            return bank[3]

        def rank_bank(h, w):
            return bank[(4, 6)[h] + w]

        def mask_bank(s):
            return bank[6 + s]

        def weight_bank(h, s):
            return bank[(4, 6)[h] + s]

        def logit_psum(h):
            return rank_bank(h, 1)[0:GR, HT:HT + GROUPS * EXPERTS]

        def group_rows(g):
            return min(GR, HT - g * GR)

        block = ctx.enter_context(nc.Block())

        @block.sync
        def _(sp):
            for i, name in enumerate(NAMES):
                if i >= EARLY + STAGES:
                    sp.wait_ge(hi_done, i - STAGES + 1)
                    sp.wait_ge(lo_done[NAMES[i - STAGES]], 1)
                slot, src, _parts = load_at[name]
                sp.dma_start(slot, src).then_inc(loaded[place_of(i)[0]], 16)
                if name == f"x0_{len(PIECES[0]) - 2}":
                    sp.dma_start(table_sb[:], table).then_inc(s_table, 16)
                elif name == "x1_1":
                    sp.dma_start(cst[:], const).then_inc(s_const, 16)
            for h in range(HALVES):
                sp.wait_ge(y_act, h + 1)
                sp.dma_start(out[:, h, 0, :], yT[:, 0, :]).then_inc(s_out, 16)
                sp.wait_ge(y_dve, h + 1)
                sp.dma_start(out[:, h, 1, :], yT[:, 1, :]).then_inc(s_out, 16)
            sp.wait_ge(s_out, 16 * KD * HALVES)

        @block.gpsimd
        def _(pool):
            def inv_std(n):
                for g in range(GROUPS):
                    pool.wait_ge(spread_ready, GROUPS * n + g + 1)
                    nc.gpsimd.tensor_tensor(rstd[:, n % 2, g:g + 1], spread[:, n % 2, g:g + 1], minus_half[:, 0:1],
                                            ALU.pow).then_inc(rstd_ready, 1)

            def lo_part(name):
                pool.wait_ge(hi_done, NAMES.index(name) + 1)
                slot, _src, (hi, lo) = load_at[name]
                nc.gpsimd.tensor_tensor(lo, slot, as_f32(hi), ALU.subtract).then_inc(lo_done[name], 1)

            def embed_rows():
                pool.wait_ge(s_rows, 1)
                for g in range(GROUPS):
                    pool.wait_ge(tok_copied, g + 1)
                    nc.gpsimd.tensor_tensor(resid[1][:, g, :], resid[1][:, g, :], table_sb[:, 0, :],
                                            ALU.add).then_inc(resid_ready, 1)

            def rotated(h, s):
                pool.wait_ge(rot_read, 8 * h + 4 * (s + 1))
                nc.gpsimd.tensor_tensor(rot[s][0][:], rot[s][0][:], rot[s][1][:], ALU.subtract).then_inc(rot_ready[s], 1)
                nc.gpsimd.tensor_tensor(rot[s][2][:], rot[s][2][:], rot[s][3][:], ALU.add).then_inc(rot_ready[s], 1)

            def qk_lo_part(h, s):
                for parity in range(2):
                    pool.wait_ge(qk_hi, 4 * h + 2 * s + parity + 1)
                    at = (2 * parity + s) * HPE
                    nc.gpsimd.tensor_tensor(qk[1][:, at:at + HT], rot[s][2 * parity][:],
                                            as_f32(qk[0][:, at:at + HT]), ALU.subtract).then_inc((queries_lo, keys_lo)[s], 1)

            def second_mask(h):
                pool.wait_ge(slot_in_ready, 4 * (h + 1))
                nc.gpsimd.tensor_tensor(mask[h][:, 1, :], mask[h][:, 1, :], mask[h][:, 0, :],
                                        ALU.add).then_inc(mask2_ready, 1)

            def weigh_slot(n, slot):
                pool.wait_ge(weight_ready, 2 * (n // FT + 1))
                pool.wait_ge((act1, act2)[slot], n + 1)
                at = act_ring[:, n % 2, slot, :]
                nc.gpsimd.tensor_tensor(at, at, weight[:, slot, :], ALU.mult).then_inc(actw, 1)

            def mix(n):
                for slot in range(2):
                    weigh_slot(n, slot)
                pool.wait_ge(actw, 2 * (n + 1))
                if n >= 2:
                    pool.wait_ge(mix_hi, n - 1)
                    pool.wait_ge(mix_lo, n - 1)
                nc.gpsimd.tensor_tensor(mix_ring[:, n % 2, :], act_ring[:, n % 2, 0, :],
                                        act_ring[:, n % 2, 1, :], ALU.add).then_inc(mixed, 1)

            nc.gpsimd.memset(as_f32(zeros), 0.0).then_inc(s_zeros, 1)
            nc.gpsimd.memset(minus_half[:], -0.5).then_inc(s_mhalf, 1)
            pool.wait_ge(s_mhalf, 1)
            for i in range(len(PIECES[0]) - 1):
                lo_part(f"w{i}")
            lo_part("x1_0")
            inv_std(0)
            lo_part("q_w")
            lo_part("k_w")
            pool.wait_ge(tok_mm, GROUPS)
            for i in range(4):
                for part in qk:
                    last = nc.gpsimd.memset(as_f32(part[:, i * HPE + HT:(i + 1) * HPE]), 0.0)
            last.then_inc(s_pads, 1)
            lo_part("x1_2")
            rotated(0, 0)
            qk_lo_part(0, 0)
            embed_rows()
            inv_std(1)
            lo_part("rest_w")
            inv_std(2)
            lo_part("ffn1")
            rotated(1, 0)
            qk_lo_part(1, 0)
            rotated(1, 1)
            qk_lo_part(1, 1)
            lo_part("ffn2")
            lo_part("ffn3")
            for n in range(NS - 1):
                mix(n)
                if n == 2:
                    inv_std(3)
                elif n == 1:
                    second_mask(0)
                elif n in (3, 4):
                    lo_part(f"ffn{n + 3}")
                elif n == 7:
                    second_mask(1)
                if n == NS - 2:
                    weigh_slot(n + 1, 0)

        @block.scalar
        def _(act):
            act.wait_ge(s_mhalf, 1)
            nc.scalar.activation(neg_top[:], minus_half[:], ACT.Exp).then_inc(s_warm, 1)

            def hi_part(name):
                i = NAMES.index(name)
                at, count = place_of(i)
                act.wait_ge(loaded[at], 16 * count)
                if name == f"ffn{EARLY_IN[0]}":
                    for first in NAMES[:EARLY]:
                        act.wait_ge(lo_done[first], 1)
                slot, _src, (hi, _lo) = load_at[name]
                nc.scalar.activation(hi, slot, ACT.Copy).then_inc(hi_done, 1)

            def embed_copy():
                for g in range(GROUPS):
                    act.wait_ge(tok_mm, GROUPS + max(g + 1, 2))
                    nc.scalar.activation(resid[1][:, g, :], tok_psum(1, g), ACT.Copy).then_inc(tok_copied, 1)

            def normalise(n):
                act.wait_ge(shift_ready, n // 2 + 1)
                for g in range(GROUPS):
                    nc.scalar.activation(xnorm[1][:, g, :], resid[1][:, g, :], ACT.Identity, bias=shift[:, g:g + 1],
                                         scale=rstd[:, 1, g:g + 1]).then_inc(xnorm_ready, 1)

            def xT_hi_part(n):
                act.wait_ge(xT_mm, n + 1)
                for k in range(KD):
                    nc.scalar.activation(xT[n % 2][0][:, k * HPE:k * HPE + HP], xT_bank(n, k)[:, 0:HP],
                                         ACT.Copy).then_inc(xT_hi, 1)

            def v_hi_part(h):
                act.wait_ge(v_mm, h + 1)
                if h:
                    act.wait_ge(pv_mm, GROUPS * h)
                for g in range(GROUPS):
                    nc.scalar.activation(val[0][0:GR, g * D:(g + 1) * D], v_bank(h, g), ACT.Copy).then_inc(v_hi, 1)

            def qk_hi_part(h, s):
                if h and s == 0:
                    act.wait_ge(s_mm, h)
                for parity in range(2):
                    act.wait_ge(rot_ready[s], 2 * h + parity + 1)
                    at = (2 * parity + s) * HPE
                    nc.scalar.activation(qk[0][:, at:at + HT], rot[s][2 * parity][:], ACT.Copy).then_inc(qk_hi, 1)

            def exp_scores(h):
                act.wait_ge(s_negtop, h + 1)
                if h:
                    act.wait_ge(inv_ready, h)
                for g in range(GROUPS):
                    nc.scalar.activation(scores[:, g, :], scores[:, g, :], ACT.Exp, bias=neg_top[:, g:g + 1],
                                         accum_out=total[:, g:g + 1]).then_inc(p_ready, 1)

            def pT_hi_part(h):
                act.wait_ge(pT_mm, h + 1)
                if h:
                    act.wait_ge(pv_mm, GROUPS * h)
                nc.scalar.activation(probsT[0][0:GR, :], pT_bank()[0:GR, 0:HP], ACT.Copy).then_inc(pT_hi, 1)

            def ranks_copy(h):
                act.wait_ge(ranks_mm, h + 1)
                if h:
                    act.wait_ge(slot_in_ready, 4 * h)
                for w in range(2):
                    nc.scalar.activation(ranks[:, w, :], rank_bank(h, w)[:, 0:HT], ACT.Copy).then_inc(ranks_ready, 1)

            def gap_to_tanh(h):
                act.wait_ge(gap_ready, h + 1)
                nc.scalar.activation(gap_tanh[:], gap[:], ACT.Tanh, scale=0.5).then_inc(tanh_ready, 1)

            def mask_copy(h):
                act.wait_ge(mask_mm, h + 1)
                for s in range(2):
                    nc.scalar.activation(mask[h][:, s, :], mask_bank(s)[:, 0:HT], ACT.Copy,
                                         scale=LORA_SCALE).then_inc(mask_ready, 1)

            def weight_copy(h):
                act.wait_ge(weight_mm, h + 1)
                if h:
                    act.wait_ge(actw, 2 * FT)
                for s in range(2):
                    nc.scalar.activation(weight[:, s, :], weight_bank(h, s)[:, 0:HT], ACT.Copy).then_inc(weight_ready, 1)

            def slot_hi_part(h):
                if h:
                    act.wait_ge(up2_mm, FT)
                for s in range(2):
                    for w in range(2):
                        act.wait_ge(slot_in_ready, 4 * h + 2 * s + w + 1)
                        at = slice((2 * s + w) * HT, (2 * s + w + 1) * HT)
                        nc.scalar.activation(slot_inr[0][:, at], slot_in[:, s, w, :], ACT.Copy).then_inc(slot_hi, 1)

            def silu(n, slot):
                if slot == 0:
                    act.wait_ge(gate1_mm, n + 1)
                    if n >= 2:
                        act.wait_ge(mixed, n - 1)
                        act.wait_ge(act_lo, 2 * (n - 1))
                else:
                    act.wait_ge(gate2_mm, n + 1)
                nc.scalar.activation(act_ring[:, n % 2, slot, :], up_bank(n, 0)[:, 0:HT],
                                     ACT.Silu).then_inc((silu1, silu2)[slot], 1)

            def hi_parts(n):
                if n >= 2:
                    act.wait_ge(down_mm, n - 1)
                for slot in range(2):
                    if (n, slot) == (NS - 1, 1):
                        act.wait_ge(last_actw, 1)
                    else:
                        act.wait_ge(actw, 2 * n + slot + 1)
                    nc.scalar.activation(actr[n % 2][0][:, slot * HT:(slot + 1) * HT], act_ring[:, n % 2, slot, :],
                                         ACT.Copy).then_inc(act_hi, 1)
                act.wait_ge(mixed, n + 1)
                nc.scalar.activation(mixr[n % 2][0][:], mix_ring[:, n % 2, :], ACT.Copy).then_inc(mix_hi, 1)

            def low_hi_part(h):
                act.wait_ge(low_ready, h + 1)
                nc.scalar.activation(lowr[0][:], low_sum, ACT.Copy).then_inc(low_hi, 1)

            def y_copy(h):
                act.wait_ge(y_mm, KD * h + 1)
                nc.scalar.activation(yT[:, 0, :], y_bank(h, 0)[:, 0:HT], ACT.Copy).then_inc(y_act, 1)

            for name in NAMES[:NAMES.index("x1_0")]:
                hi_part(name)
            hi_part("x1_0")
            hi_part("x1_1")
            hi_part("q_w")
            hi_part("k_w")
            xT_hi_part(0)
            hi_part("valout")
            hi_part("x1_2")
            hi_part("rest_w")
            act.wait_ge(s_pads, 1)
            qk_hi_part(0, 0)
            act.wait_ge(vo_mm, 1)
            nc.scalar.activation(vo[0][:], vo_bank[:, :], ACT.Copy).then_inc(vo_hi, 1)
            qk_hi_part(0, 1)
            hi_part("ffn0")
            embed_copy()
            exp_scores(0)
            v_hi_part(0)
            pT_hi_part(0)
            normalise(1)
            hi_part("ffn1")
            xT_hi_part(1)
            hi_part("ffn2")
            hi_part("ffn3")
            xT_hi_part(2)
            hi_part("ffn4")
            qk_hi_part(1, 0)
            hi_part("ffn5")
            ranks_copy(0)
            qk_hi_part(1, 1)
            mask_copy(0)
            slot_hi_part(0)
            gap_to_tanh(0)
            hi_part("ffn6")
            exp_scores(1)
            weight_copy(0)
            for n in range(NS + 1):
                if n == FT:
                    slot_hi_part(1)
                if n < NS:
                    silu(n, 0)
                if n >= 1:
                    hi_parts(n - 1)
                if n == FT:
                    weight_copy(1)
                if n == 0:
                    v_hi_part(1)
                if n < NS:
                    silu(n, 1)
                if n == 0:
                    pT_hi_part(1)
                    hi_part("ffn7")
                elif n == 3:
                    normalise(3)
                elif n == 4:
                    xT_hi_part(3)
                elif n == 6:
                    gap_to_tanh(1)
                    ranks_copy(1)
                    mask_copy(1)
                elif n == FT + 1:
                    low_hi_part(0)
                elif n == FT + 2:
                    y_copy(0)
            low_hi_part(1)
            y_copy(1)

        @block.vector
        def _(dve):
            chain = [0]

            def link(ins):
                chain[0] += 1
                ins.then_inc(s_chain, 1)
                dve.wait_ge(s_chain, chain[0])

            def lo_part(name):
                dve.wait_ge(hi_done, NAMES.index(name) + 1)
                slot, _src, (hi, lo) = load_at[name]
                nc.vector.tensor_tensor(lo, slot, as_f32(hi), ALU.subtract).then_inc(lo_done[name], 1)

            def moments_behind(h, n, g, written):
                if 1 <= g <= GROUPS:
                    dve.wait_ge(written, GROUPS * h + g)
                    nc.vector.bn_stats(stats[:, n % 2, g - 1, :], resid[h][:, g - 1, :]).then_inc(stats_ready, 1)
                if g >= 2:
                    dve.wait_ge(stats_ready, GROUPS * n + g - 1)
                    if n >= 2:
                        dve.wait_ge(xnorm_ready, GROUPS * (n - 1))
                    nc.vector.bn_aggr(moments[:, n % 2, g - 2, :], stats[:, n % 2, g - 2, :]).then_inc(moments_ready, 1)
                    dve.wait_ge(moments_ready, GROUPS * n + g - 1)
                    nc.vector.tensor_scalar(spread[:, n % 2, g - 2:g - 1], moments[:, n % 2, g - 2, 1:2], EPS, None,
                                            ALU.add).then_inc(spread_ready, 1)

            def shift_of(n):
                dve.wait_ge(rstd_ready, GROUPS * (n + 1))
                nc.vector.scalar_tensor_tensor(out=shift[:], in0=moments[:, n % 2, :, 0], scalar=-1.0,
                                               in1=rstd[:, n % 2, :], op0=ALU.mult, op1=ALU.mult).then_inc(shift_ready, 1)

            def normalise(h, n):
                if n >= 2:
                    dve.wait_ge(xT_mm, n - 1)
                for g in range(GROUPS):
                    dve.wait_ge(rstd_ready, GROUPS * n + g + 1)
                    nc.vector.tensor_scalar(xnorm[n % 2][:, g, :], resid[h][:, g, :], moments[:, n % 2, g, 0:1],
                                            rstd[:, n % 2, g:g + 1], ALU.subtract, ALU.mult).then_inc(xnorm_ready, 1)

            def embed_rows(h):
                for g in range(GROUPS + 2):
                    if g < GROUPS and h == 0:
                        dve.wait_ge(tok_mm, g + 1)
                        nc.vector.tensor_tensor(resid[0][:, g, :], tok_psum(0, g), table_sb[:, 0, :],
                                                ALU.add).then_inc(resid_ready, 1)
                    moments_behind(h, h, g, resid_ready)

            def xT_lo_part(n):
                for k in range(KD):
                    dve.wait_ge(xT_hi, KD * n + k + 1)
                    at = slice(k * HPE, k * HPE + HP)
                    nc.vector.tensor_tensor(xT[n % 2][1][:, at], xT_bank(n, k)[:, 0:HP],
                                            as_f32(xT[n % 2][0][:, at]), ALU.subtract).then_inc(xT_lo, 1)

            def rotate(h, s):
                if h:
                    dve.wait_ge((queries_lo, keys_lo)[s], 2 * h)
                for i, parity, at in ((0, 0, C_COS), (2, 0, C_SIN), (1, 1, C_SIN), (3, 1, C_COS)):
                    dve.wait_ge(qk_mm, 4 * h + 2 * s + parity + 1)
                    factor = cst[:, at:at + ROWS].unsqueeze(1).to_broadcast([P, HALF_IMAGES, ROWS])
                    nc.vector.tensor_tensor(rot[s][i][:].rearrange("p (b t) -> p b t", t=ROWS),
                                            rope_bank(s, parity)[:, 0:HT].rearrange("p (b t) -> p b t", t=ROWS),
                                            factor, ALU.mult).then_inc(rot_read, 1)

            def rotated_keys(h):
                dve.wait_ge(rot_read, 8 * (h + 1))
                nc.vector.tensor_tensor(rot[1][0][:], rot[1][0][:], rot[1][1][:], ALU.subtract).then_inc(rot_ready[1], 1)
                nc.vector.tensor_tensor(rot[1][2][:], rot[1][2][:], rot[1][3][:], ALU.add).then_inc(rot_ready[1], 1)

            def keys_lo_part():
                for parity in range(2):
                    dve.wait_ge(qk_hi, 3 + parity)
                    at = (2 * parity + 1) * HPE
                    nc.vector.tensor_tensor(qk[1][:, at:at + HT], rot[1][2 * parity][:],
                                            as_f32(qk[0][:, at:at + HT]), ALU.subtract).then_inc(keys_lo, 1)

            def v_lo_part(h):
                for g in range(GROUPS):
                    dve.wait_ge(v_hi, GROUPS * h + max(g + 1, 2))
                    at = slice(g * D, (g + 1) * D)
                    nc.vector.tensor_tensor(val[1][0:GR, at], v_bank(h, g), as_f32(val[0][0:GR, at]),
                                            ALU.subtract).then_inc(v_lo, 1)

            def mask_scores(h):
                dve.wait_ge(s_mm, h + 1)
                if h:
                    dve.wait_ge(pT_mm, h)
                nc.vector.scalar_tensor_tensor(
                    out=scores[:], in0=score_bank()[0:GR, 0:GROUPS * GRE].rearrange("p (g t) -> p g t", t=GRE),
                    scalar=SCORE_SCALE, in1=cst[0:GR, C_MASK:C_MASK + GRE].unsqueeze(1).to_broadcast([GR, GROUPS, GRE]),
                    op0=ALU.mult, op1=ALU.add).then_inc(s_masked, 1)
                dve.wait_ge(s_masked, h + 1)
                dve.wait_ge(s_warm, 1)
                nc.vector.tensor_reduce(neg_top[:], scores[:], AX_X, ALU.max, negate=True).then_inc(s_negtop, 1)

            def inv_sums(h):
                dve.wait_ge(p_ready, GROUPS * (h + 1))
                if h:
                    dve.wait_ge(h2_ready, GROUPS * h)
                nc.vector.reciprocal(inv_total[:], total[:]).then_inc(inv_ready, 1)

            def pT_lo_part(h):
                dve.wait_ge(pT_hi, h + 1)
                nc.vector.tensor_tensor(probsT[1][0:GR, :], pT_bank()[0:GR, 0:HP], as_f32(probsT[0][0:GR, :]),
                                        ALU.subtract).then_inc(pT_lo, 1)

            def add_attention(h, steps=range(GROUPS + 2)):
                dve.wait_ge(inv_ready, h + 1)
                for g in steps:
                    if g < GROUPS:
                        dve.wait_ge(pv_mm, GROUPS * h + max(g + 1, 2))
                        nc.vector.scalar_tensor_tensor(out=resid[h][:, g, :], in0=v_bank(h, g),
                                                       scalar=inv_total[:, g:g + 1], in1=resid[h][:, g, :],
                                                       op0=ALU.mult, op1=ALU.add).then_inc(h2_ready, 1)
                    moments_behind(h, 2 + h, g, h2_ready)

            def choose(h):
                dve.wait_ge(gate_mm, h + 1)
                nc.vector.tensor_copy(logits[:].rearrange("p g e -> p (g e)"), logit_psum(h)).then_inc(logits_ready, 1)
                dve.wait_ge(logits_ready, h + 1)
                all_pairs = [GR, GROUPS, EXPERTS, EXPERTS]
                nc.vector.tensor_reduce(best[:, 0, :], logits[:], AX_X, ALU.max).then_inc(s_chain, 1)
                chain[0] += 1
                link(nc.vector.tensor_tensor(versus[:], logits[:].unsqueeze(2).to_broadcast(all_pairs),
                                             logits[:].unsqueeze(3).to_broadcast(all_pairs), ALU.subtract))
                order = cst[0:GR, C_ORDER:C_ORDER + EXPERTS * EXPERTS]
                link(nc.vector.tensor_tensor(versus[:].rearrange("p g e j -> p g (e j)"),
                                             versus[:].rearrange("p g e j -> p g (e j)"),
                                             order.unsqueeze(1).to_broadcast([GR, GROUPS, EXPERTS * EXPERTS]), ALU.is_ge))
                link(nc.vector.tensor_reduce(place[:], versus[:], AX_X, ALU.add))
                if h:
                    dve.wait_ge(mask_mm, h)
                places = place[:].unsqueeze(3).to_broadcast([GR, GROUPS, EXPERTS, RANK])
                nc.vector.tensor_scalar(chosen_x[:, 0], places, 0.0, None, ALU.is_equal).then_inc(chosen_ready, 1)
                dve.wait_ge(chosen_ready, 2 * h + 1)
                nc.vector.scalar_tensor_tensor(out=chosen_x[:, 1], in0=places, scalar=1.0, in1=chosen_x[:, 0],
                                               op0=ALU.is_equal, op1=ALU.subtract).then_inc(chosen_ready, 1)
                link(nc.vector.scalar_tensor_tensor(out=second[:], in0=place[:], scalar=1.0, in1=logits[:],
                                                    op0=ALU.is_equal, op1=ALU.mult))
                link(nc.vector.tensor_reduce(best[:, 1, :], second[:], AX_X, ALU.add))
                if h:
                    dve.wait_ge(tanh_ready, h)
                nc.vector.tensor_tensor(gap[:], best[:, 0, :], best[:, 1, :], ALU.subtract).then_inc(gap_ready, 1)

            def weigh(h):
                dve.wait_ge(tanh_ready, h + 1)
                for s, sign in enumerate((0.5, -0.5)):
                    nc.vector.tensor_scalar(slot_w[:, s, :], gap_tanh[:], sign, 0.5, ALU.mult, ALU.add).then_inc(s_chain, 1)
                chain[0] += 2
                dve.wait_ge(s_chain, chain[0])
                if h:
                    dve.wait_ge(weight_mm, h)
                nc.vector.tensor_copy(slot_wx[:], slot_w[:].unsqueeze(3).to_broadcast([GR, 2, GROUPS, P])).then_inc(slots_ready, 1)

            def slot_inputs(h, s):
                dve.wait_ge(mask_ready, 2 * h + s + 1)
                for w in range(2):
                    dve.wait_ge(ranks_ready, 2 * h + w + 1)
                    nc.vector.tensor_tensor(slot_in[:, s, w, :], ranks[:, w, :], mask[h][:, s, :],
                                            ALU.mult).then_inc(slot_in_ready, 1)

            def slot_lo_part(h, s):
                for w in range(2):
                    dve.wait_ge(slot_hi, 4 * h + 2 * s + w + 1)
                    at = slice((2 * s + w) * HT, (2 * s + w + 1) * HT)
                    nc.vector.tensor_tensor(slot_inr[1][:, at], slot_in[:, s, w, :], as_f32(slot_inr[0][:, at]),
                                            ALU.subtract).then_inc(slot_lo, 1)

            def gated(n, slot):
                if slot == 0:
                    dve.wait_ge(silu1, n + 1)
                    dve.wait_ge(up1_mm, n + 1)
                else:
                    dve.wait_ge(silu2, n + 1)
                    dve.wait_ge(up2_mm, n + 1)
                at = act_ring[:, n % 2, slot, :]
                nc.vector.tensor_tensor(at, up_bank(n, 1)[:, 0:HT], at, ALU.mult).then_inc((act1, act2)[slot], 1)

            def lo_parts(n):
                if n >= 2:
                    dve.wait_ge(down_mm, n - 1)
                for slot in range(2):
                    dve.wait_ge(act_hi, 2 * n + slot + 1)
                    at = slice(slot * HT, (slot + 1) * HT)
                    nc.vector.tensor_tensor(actr[n % 2][1][:, at], act_ring[:, n % 2, slot, :],
                                            as_f32(actr[n % 2][0][:, at]), ALU.subtract).then_inc(act_lo, 1)
                dve.wait_ge(mix_hi, n + 1)
                nc.vector.tensor_tensor(mixr[n % 2][1][:], mix_ring[:, n % 2, :], as_f32(mixr[n % 2][0][:]),
                                        ALU.subtract).then_inc(mix_lo, 1)

            def last_mix():
                n = NS - 1
                dve.wait_ge(act2, n + 1)
                at = act_ring[:, n % 2, :, :]
                nc.vector.tensor_tensor(at[:, 1, :], at[:, 1, :], weight[:, 1, :], ALU.mult).then_inc(last_actw, 1)
                dve.wait_ge(actw, 2 * n + 1)
                dve.wait_ge(last_actw, 1)
                nc.vector.tensor_tensor(mix_ring[:, n % 2, :], at[:, 0, :], at[:, 1, :], ALU.add).then_inc(mixed, 1)

            def low_sums(h):
                dve.wait_ge(slot_lo, 4 * HALVES)
                dve.wait_ge(mask2_ready, h + 1)
                if h:
                    dve.wait_ge(s_out, 16 * KD * h)
                for s in range(2):
                    dve.wait_ge(low_mm, 2 * h + s + 1)
                    nc.vector.tensor_tensor(low[:, s, :], low_bank[s][:, 0:HT], mask[h][:, s, :],
                                            ALU.mult).then_inc(low_masked, 1)
                dve.wait_ge(low_masked, 2 * (h + 1))
                if h:
                    dve.wait_ge(low_lo, h)
                nc.vector.tensor_tensor(low_sum, low[:, 0, :], low[:, 1, :], ALU.add).then_inc(low_ready, 1)

            def low_lo_part(h):
                dve.wait_ge(low_hi, h + 1)
                nc.vector.tensor_tensor(lowr[1][:], low_sum, as_f32(lowr[0][:]), ALU.subtract).then_inc(low_lo, 1)

            def y_copy(h):
                dve.wait_ge(y_mm, KD * (h + 1))
                nc.vector.tensor_copy(yT[:, 1, :], y_bank(h, 1)[:, 0:HT]).then_inc(y_dve, 1)

            for i in range(len(PIECES[0]) - 1):
                lo_part(f"x0_{i}")
            dve.wait_ge(s_table, 16)
            nc.vector.tensor_tensor(table_sb[:, 0, :], table_sb[:, 0, :], table_sb[:, 1, :], ALU.add).then_inc(s_rows, 1)
            dve.wait_ge(s_rows, 1)
            embed_rows(0)
            normalise(0, 0)
            lo_part("x1_1")
            xT_lo_part(0)
            lo_part("valout")
            rotate(0, 0)
            rotate(0, 1)
            rotated_keys(0)
            keys_lo_part()
            dve.wait_ge(vo_hi, 1)
            nc.vector.tensor_tensor(vo[1][:], vo_bank[:, :], as_f32(vo[0][:]), ALU.subtract).then_inc(vo_lo, 1)
            lo_part("ffn0")
            mask_scores(0)
            embed_rows(1)
            v_lo_part(0)
            inv_sums(0)
            pT_lo_part(0)
            shift_of(1)
            add_attention(0, range(GROUPS))
            xT_lo_part(1)
            add_attention(0, range(GROUPS, GROUPS + 2))
            dve.wait_ge(s_const, 16)
            nc.vector.tensor_copy(ident_bf[:], ident).then_inc(s_ident, 1)
            normalise(0, 2)
            rotate(1, 0)
            xT_lo_part(2)
            rotate(1, 1)
            choose(0)
            slot_inputs(0, 0)
            slot_inputs(0, 1)
            slot_lo_part(0, 0)
            weigh(0)
            mask_scores(1)
            slot_lo_part(0, 1)
            lo_part("ffn4")
            lo_part("ffn5")
            for n in range(NS + 1):
                if n == FT:
                    slot_lo_part(1, 0)
                    slot_lo_part(1, 1)
                if n < NS:
                    gated(n, 0)
                if n >= 1:
                    lo_parts(n - 1)
                if n == 0:
                    v_lo_part(1)
                if n < NS:
                    gated(n, 1)
                if n == NS - 1:
                    last_mix()
                if n == 0:
                    inv_sums(1)
                    pT_lo_part(1)
                elif n == 2:
                    add_attention(1)
                elif n == 3:
                    shift_of(3)
                elif n == 4:
                    xT_lo_part(3)
                elif n == 5:
                    choose(1)
                elif n == 6:
                    weigh(1)
                elif n == 7:
                    slot_inputs(1, 0)
                    slot_inputs(1, 1)
                elif n == FT + 1:
                    low_sums(0)
                    low_lo_part(0)
                elif n == FT + 2:
                    y_copy(0)
            low_sums(1)
            low_lo_part(1)
            y_copy(1)

        @block.tensor
        def _(pe):
            def product(dst, w, x, start, stop, open_bank=False):
                nc.tensor.matmul(dst, w[0], x[0], start=start, stop=False, skip_group_check=open_bank)
                nc.tensor.matmul(dst, w[0], x[1], start=False, stop=False, skip_group_check=open_bank)
                return nc.tensor.matmul(dst, w[1], x[0], start=False, stop=stop, skip_group_check=open_bank)

            def cols(parts, a, b, rows=P):
                return [p[0:rows, a:b] for p in parts]

            def split(name):
                pe.wait_ge(hi_done, NAMES.index(name) + 1)
                pe.wait_ge(lo_done[name], 1)

            def embedding(h, tiles):
                order = [(k, g) for k in tiles for g in range(GROUPS)]
                if h == 0 and KX - 1 in tiles:
                    order = [(k, g) for g in range(GROUPS) for k in tiles]
                for i, (k, g) in enumerate(order):
                    if i == order.index((k, 0)):
                        if k in PIECES[h]:
                            split(f"x{h}_{PIECES[h].index(k)}")
                        if k in PIECES[0]:
                            split(f"w{PIECES[0].index(k)}")
                    at = k * HP + g * GR
                    last = product(tok_psum(h, g), cols(xhalf[h], at, at + GR),
                                   cols(embed, k * D, (k + 1) * D), k == 0 and (h, g) != (1, 1), k == KX - 1, h == 1)
                    if k == KX - 1:
                        last.then_inc(tok_mm, 1)

            def value_out():
                split("valout")
                pe.wait_ge(xT_lo, KD)
                for m in range(KD):
                    for k in range(KD):
                        last = product(vo_bank[:, m * D:(m + 1) * D], cols(valout, k * D + m * P, k * D + (m + 1) * P),
                                       cols(valout, (KD + k) * D, (KD + k + 1) * D), k == 0, k == KD - 1)
                last.then_inc(vo_mm, 1)

            def transpose_rows(n):
                pe.wait_ge(s_const, 16)
                pe.wait_ge(resid_ready, GROUPS * HALVES if n else GROUPS)
                if n == 2:
                    pe.wait_ge(h2_ready, GROUPS)
                elif n == 3:
                    pe.wait_ge(h2_ready, GROUPS * HALVES)
                for g in range(GROUPS):
                    pe.wait_ge(xnorm_ready, GROUPS * n + g + 1)
                    for k in range(KD):
                        last = nc.tensor.transpose(xT_bank(n, k)[:, g * GR:(g + 1) * GR],
                                                   xnorm[n % 2][:, g, k * P:(k + 1) * P], ident[0:GR, 0:GR])
                last.then_inc(xT_mm, 1)

            def queries_keys(h, s):
                split(("q_w", "k_w")[s])
                pe.wait_ge(xT_lo, KD * (h + 1))
                if h == 0:
                    pe.wait_ge(resid_ready, GROUPS)
                elif s == 0:
                    pe.wait_ge(rot_read, 4)
                else:
                    pe.wait_ge(s_masked, 1)
                    pe.wait_ge(pT_lo, 1)
                for parity in range(2):
                    for k in range(KD):
                        at = M_QK + ((s * KD + k) * 2 + parity) * P
                        last = product(rope_bank(s, parity)[:, 0:HT], cols(small, at, at + P),
                                       cols(xT[h], k * HPE, k * HPE + HT), k == 0, k == KD - 1)
                    last.then_inc(qk_mm, 1)

            def values(h):
                pe.wait_ge(vo_lo, 1)
                if h == 0:
                    pe.wait_ge(xT_lo, KD)
                else:
                    pe.wait_ge(mask_ready, 2)
                for g in range(GROUPS):
                    for k in range(KD):
                        at = k * HPE + g * GR
                        last = product(v_bank(h, g), cols(xT[h], at, at + GR), cols(vo, k * D, (k + 1) * D),
                                       k == 0, k == KD - 1)
                last.then_inc(v_mm, 1)

            def score(h):
                pe.wait_ge(queries_lo, 2 * (h + 1))
                pe.wait_ge(keys_lo, 2 * (h + 1))
                pe.wait_ge(s_pads, 1)
                pe.wait_ge(rot_read, 8 * (h + 1))
                for g in range(GROUPS):
                    for k in range(KD):
                        q, key = 2 * k * HPE + g * GR, (2 * k + 1) * HPE + g * GR
                        last = product(score_bank()[0:GR, g * GRE:(g + 1) * GRE], cols(qk, q, q + GR),
                                       cols(qk, key, key + GRE), k == 0, k == KD - 1)
                last.then_inc(s_mm, 1)

            def transpose_probs(h):
                pe.wait_ge(p_ready, GROUPS * (h + 1))
                for g in range(GROUPS):
                    last = nc.tensor.transpose(pT_bank()[0:GR, g * GR:(g + 1) * GR], scores[:, g, 0:GR],
                                               ident[0:GR, 0:GR])
                last.then_inc(pT_mm, 1)

            def weighted_values(h):
                pe.wait_ge(pT_lo, h + 1)
                for g in range(GROUPS):
                    pe.wait_ge(v_lo, GROUPS * h + max(g + 1, 2))
                    last = product(v_bank(h, g), cols(probsT, g * GR, (g + 1) * GR, GR),
                                   cols(val, g * D, (g + 1) * D, GR), True, True)
                    last.then_inc(pv_mm, 1)

            def router(h):
                split("rest_w")
                pe.wait_ge(xT_lo, KD * (h + 3))
                if h == 0:
                    pe.wait_ge(xT_lo, 2 * KD)
                x = xT[h]
                for g in range(GROUPS):
                    for k in range(KD):
                        at, gt = k * HPE + g * GR, M_GATE + k * EXPERTS
                        last = product(logit_psum(h)[:, g * EXPERTS:(g + 1) * EXPERTS], cols(x, at, at + GR),
                                       cols(small, gt, gt + EXPERTS), k == 0, k == KD - 1)
                last.then_inc(gate_mm, 1)

            def rank_products(h):
                x = xT[h]
                for w in range(2):
                    if w == 1:
                        pe.wait_ge(logits_ready, h + 1)
                    for k in range(KD):
                        at = M_A13 + (k * 2 + w) * P
                        last = product(rank_bank(h, w)[:, 0:HT], cols(small, at, at + P),
                                       cols(x, k * HPE, k * HPE + HT), k == 0, k == KD - 1)
                last.then_inc(ranks_mm, 1)

            def spread_masks(h):
                pe.wait_ge(chosen_ready, 2 * (h + 1))
                pe.wait_ge(s_ident, 1)
                if h == 0:
                    pe.wait_ge(rot_read, 12)
                else:
                    pe.wait_ge(ranks_ready, 2 * (h + 1))
                for s in range(2):
                    for g in range(GROUPS):
                        rows = group_rows(g)
                        last = nc.tensor.matmul(mask_bank(s)[:, g * GR:g * GR + rows],
                                                chosen_x[:, s, g].rearrange("p e r -> p (e r)"), ident_bf[0:GR, 0:rows],
                                                start=True, stop=True)
                last.then_inc(mask_mm, 1)

            def spread_weights(h):
                pe.wait_ge(slots_ready, h + 1)
                if h == 0:
                    pe.wait_ge(ranks_ready, 2)
                else:
                    pe.wait_ge(mask_ready, 2 * (h + 1))
                for s in range(2):
                    for g in range(GROUPS):
                        rows = group_rows(g)
                        last = nc.tensor.transpose(weight_bank(h, s)[:, g * GR:g * GR + rows], slot_wx[0:rows, s, g, :],
                                                   ident[0:rows, 0:rows])
                last.then_inc(weight_mm, 1)

            def ffn_cols(t, at):
                return cols(ffn[t], at, at + P)

            def common(n, w):
                h, t = divmod(n, FT)
                if n == 0:
                    pe.wait_ge(xT_lo, 3 * KD)
                elif n == 1:
                    pe.wait_ge(weight_ready, 2)
                elif n == UP_PAIRS_FROM:
                    pe.wait_ge(y_act, 1)
                    pe.wait_ge(y_dve, 1)
                else:
                    pe.wait_ge((silu2, act2)[w], n if 2 < n < UP_PAIRS_FROM else n - 1)
                if h == 0 and w == 0:
                    split(f"ffn{t}")
                for k in range(KD):
                    product(up_bank(n, w)[:, 0:HT], ffn_cols(t, T_UP + (w * KD + k) * P),
                            cols(xT[h], k * HPE, k * HPE + HT), k == 0, False)

            def slot_part(n, slot, w):
                h, t = divmod(n, FT)
                if t == 0:
                    pe.wait_ge(slot_lo, 4 * h + 2 * slot + w + 1)
                if slot == 1:
                    pe.wait_ge((silu1, act1)[w], n + 1)
                x = (2 * slot + w) * HT
                product(up_bank(n, w)[:, 0:HT], ffn_cols(t, T_B13 + w * P), cols(slot_inr, x, x + HT),
                        False, True, slot == 1).then_inc(((gate1_mm, up1_mm), (gate2_mm, up2_mm))[slot][w], 1)

            def residual(h):
                if h == 0:
                    pe.wait_ge(act2, 2)
                else:
                    pe.wait_ge(weight_ready, 4)
                for m in range(KD):
                    for g in range(GROUPS):
                        rows = group_rows(g)
                        nc.tensor.matmul(y_bank(h, m)[:, g * GR:g * GR + rows], resid[h][:, g, m * P:(m + 1) * P],
                                         ident[0:GR, 0:rows], start=(g == 0), stop=False, skip_group_check=True)

            def down_ranks(n):
                h, t = divmod(n, FT)
                if t == 0:
                    if h == 0:
                        pe.wait_ge(pT_lo, 2)
                    else:
                        pe.wait_ge(low_masked, 2 * h)
                for s in range(2):
                    pe.wait_ge(act_lo, 2 * n + s + 1)
                    last = product(low_bank[s][:, 0:HT], ffn_cols(t, T_A2), cols(actr[n % 2], s * HT, (s + 1) * HT),
                                   t == 0, t == FT - 1)
                    if t == FT - 1:
                        last.then_inc(low_mm, 1)

            def down(n):
                h, t = divmod(n, FT)
                if t == 0:
                    residual(h)
                pe.wait_ge(mix_lo, n + 1)
                for m in range(KD):
                    last = product(y_bank(h, m)[:, 0:HT], ffn_cols(t, T_DOWN + m * P),
                                   cols(mixr[n % 2], 0, HT), False, False, True)
                last.then_inc(down_mm, 1)

            def low_out(h):
                pe.wait_ge(low_lo, h + 1)
                for m in range(KD):
                    at = M_B2 + m * P
                    last = product(y_bank(h, m)[:, 0:HT], cols(small, at, at + P), cols(lowr, 0, HT), False, True, True)
                    last.then_inc(y_mm, 1)

            def keep_warm(times):
                for _ in range(times):
                    nc.tensor.matmul(bank[7][:, :], zeros[:, 0:P], zeros, start=True, stop=True)

            pe.wait_ge(s_zeros, 1)
            keep_warm(WARM_UP)
            embedding(0, range(0, 4))
            embedding(0, range(4, KX))
            embedding(1, range(0, 2))
            transpose_rows(0)
            embedding(1, range(2, 3))
            queries_keys(0, 0)
            queries_keys(0, 1)
            value_out()
            embedding(1, range(3, KX))
            score(0)
            values(0)
            transpose_probs(0)
            keep_warm(4)
            weighted_values(0)
            transpose_rows(1)
            keep_warm(6)
            queries_keys(1, 0)
            transpose_rows(2)
            queries_keys(1, 1)
            router(0)
            rank_products(0)
            pe.wait_ge(rot_read, 12)
            keep_warm(3)
            spread_masks(0)
            common(0, 0)
            common(0, 1)
            score(1)
            slot_part(0, 0, 0)
            slot_part(0, 0, 1)
            spread_weights(0)
            values(1)
            common(1, 0)
            for n in range(NS + 2):
                if n == 0:
                    slot_part(0, 1, 0)
                    transpose_probs(1)
                    common(1, 1)
                    slot_part(0, 1, 1)
                elif n == 1:
                    slot_part(1, 0, 0)
                    slot_part(1, 0, 1)
                    common(2, 0)
                    weighted_values(1)
                    slot_part(1, 1, 0)
                    slot_part(1, 1, 1)
                else:
                    if n < NS:
                        if n > 2:
                            common(n, 0)
                        slot_part(n, 0, 0)
                        common(n, 1)
                        slot_part(n, 0, 1)
                        if n == 6:
                            rank_products(1)
                        slot_part(n, 1, 0)
                    down_ranks(n - 2)
                    if n < NS:
                        slot_part(n, 1, 1)
                    down(n - 2)
                if n == 4:
                    transpose_rows(3)
                elif n == 5:
                    router(1)
                elif n == 6:
                    spread_masks(1)
                elif n == 7:
                    spread_weights(1)
                elif n == FT + 2:
                    low_out(0)
            low_out(1)


def kernel(x, L0_tok_W, L0_tok_b, L0_tok_cls_token, L0_tok_pos_enc, L0_attn_wq, L0_attn_wk, L0_attn_wv, L0_attn_wo,
           L0_ffn_gate_w, L0_ffn_w_gate, L0_ffn_w_up, L0_ffn_w_down, L0_ffn_A1, L0_ffn_B1, L0_ffn_A3, L0_ffn_B3,
           L0_ffn_A2, L0_ffn_B2):
    import concourse.bacc as bacc
    from concourse.bass_utils import run_bass_kernel_spmd

    x = np.asarray(x)
    f32 = np.float32

    def tiles(a):
        return a.reshape(-1, P, a.shape[1]).transpose(1, 0, 2)

    def flat(a):
        return a.reshape(P, -1)

    rows = x.reshape(IMAGES, CHANNELS, GRID, PATCH, GRID, PATCH).transpose(0, 2, 4, 1, 3, 5)
    rows = rows.reshape(HALVES, HALF_IMAGES, ROWS - 1, KX * P)
    padded = np.zeros((HALVES, GROUPS * GROUP_IMAGES, ROWS, KX * P), f32)
    padded[:, :HALF_IMAGES, 1:] = rows
    patches = padded.reshape(HALVES, HP, KX, P).transpose(3, 0, 2, 1).reshape(P, HALVES, KX * HP)

    embed_w = flat(tiles(np.asarray(L0_tok_W).T))
    wv, wo = np.asarray(L0_attn_wv), np.asarray(L0_attn_wo)
    value_w = np.concatenate([flat(tiles(wv)), flat(tiles(wo.T))], axis=1)
    qT, kT = np.asarray(L0_attn_wq).T, np.asarray(L0_attn_wk).T
    qk = [flat(tiles(np.concatenate([w[:, 0::2], w[:, 1::2]], axis=1))) for w in (qT, kT)]
    ranks_first = lambda a: np.asarray(a).reshape(EXPERTS * RANK, -1).T
    a13 = np.concatenate([ranks_first(L0_ffn_A1), ranks_first(L0_ffn_A3)], axis=1)
    by_rank = lambda b: np.asarray(b).transpose(0, 2, 1).reshape(EXPERTS * RANK, -1)
    small_w = np.concatenate([*qk, flat(tiles(a13)), flat(tiles(np.asarray(L0_ffn_gate_w).T)),
                              by_rank(L0_ffn_B2)], axis=1)
    up = np.stack([np.asarray(L0_ffn_w_gate).T, np.asarray(L0_ffn_w_up).T])
    up = up.reshape(2, KD, P, FT, P).transpose(2, 3, 0, 1, 4).reshape(P, FT, -1)
    b13 = np.stack([by_rank(L0_ffn_B1), by_rank(L0_ffn_B3)]).reshape(2, P, FT, P).transpose(1, 2, 0, 3).reshape(P, FT, -1)
    a2 = tiles(ranks_first(L0_ffn_A2))
    dn = tiles(np.asarray(L0_ffn_w_down).T)
    ffn_w = np.concatenate([up, b13, a2, dn], axis=2)

    pos = np.tile(np.asarray(L0_tok_pos_enc)[0], (GROUP_IMAGES, 1))
    image = np.tile(np.asarray(L0_tok_b)[None, :], (ROWS, 1))
    image[0] = np.asarray(L0_tok_cls_token)[0, 0]
    table = np.stack([pos, np.tile(image, (GROUP_IMAGES, 1))], axis=1)

    const = np.zeros((P, C_ALL), f32)
    const[:, C_ID:C_ID + P] = np.eye(P, dtype=f32)
    i, j = np.arange(P)[:, None] // ROWS, np.arange(GRE)[None, :] // ROWS
    const[:, C_MASK:C_MASK + GRE] = np.where(i == j, 0.0, FAR)
    inv = (f32(1.0) / f32(10000.0) ** (np.arange(0, D, 2, dtype=f32) / f32(D))).astype(f32)
    angle = np.outer(inv, np.arange(ROWS, dtype=f32)).astype(f32)
    const[:, C_COS:C_COS + ROWS] = np.cos(angle)
    const[:, C_SIN:C_SIN + ROWS] = np.sin(angle)
    e, other = np.arange(EXPERTS)[:, None], np.arange(EXPERTS)[None, :]
    const[:, C_ORDER:] = np.where(other < e, 0.0, LEAST).astype(f32).reshape(1, -1)

    arrays = {"patches": patches, "embed_w": embed_w, "value_w": value_w, "small_w": small_w, "ffn_w": ffn_w,
              "const": const, "table": table}
    arrays = {k: np.ascontiguousarray(v) for k, v in arrays.items()}
    nc = bacc.Bacc("TRN2", target_bir_lowering=False, num_devices=1, dynamic_dma_scratch_size=1024)
    args = [nc.dram_tensor(k, v.shape, F32, kind="ExternalInput").ap() for k, v in arrays.items()]
    out = nc.dram_tensor("out", (P, HALVES, KD, HT), F32, kind="ExternalOutput").ap()
    vit_block(nc, *args, out)
    r = run_bass_kernel_spmd(nc, [arrays], core_ids=[0])
    got = r.results[0]["out"]
    return np.ascontiguousarray(got.transpose(1, 3, 2, 0).reshape(IMAGES, ROWS, D))
```
